# Optimizing a Trainium2 kernel written in Bass

```python
import numpy as np
import jax
import jax.numpy as jnp

def _softmax(x, axis=-1):
    return jax.nn.softmax(x, axis=axis)

def _gelu(x):
    return jax.nn.gelu(x, approximate=True)

def _silu(x):
    return jax.nn.silu(x)

def _sigmoid(x):
    return jax.nn.sigmoid(x)

def _layernorm(x, axis=-1, eps=1e-05):
    m = jnp.mean(x, axis=axis, keepdims=True)
    v = jnp.var(x, axis=axis, keepdims=True)
    return (x - m) / jnp.sqrt(v + eps)

def _scatter_add(tgt, idx, src, axis=0):
    return tgt.at[idx].add(src)

def _segment_sum(src, seg, n):
    return jax.ops.segment_sum(src, seg, n)
kernel_name = 'mk_cond_seq_d1_seqx_r2_43efc5'

def setup_inputs(seed: int=0):
    np.random.seed(seed)
    _w = jnp.asarray

    def _rec_inputs():
        import jax
        import jax.numpy as jnp
        _rk = jax.random.key(seed)
        x = 7.22e-05 + 1 * jax.random.normal(jax.random.fold_in(_rk, 1), (8, 512, 512), jnp.float32)
        _lenS = 512 - jax.random.randint(jax.random.fold_in(_rk, 7), (8,), 0, max(1, 512 // 4) + 1, jnp.int32)
        _lenS2 = 512 - jax.random.randint(jax.random.fold_in(_rk, 8), (8,), 0, max(1, 512 // 4) + 1, jnp.int32)
        cond_1024 = 0.0061147 + 1.02565 * jax.random.normal(jax.random.fold_in(_rk, 11), (8, 512), jnp.float32)
        return (x, cond_1024)
    x, cond_1024 = _rec_inputs()

    def _L0_cond_setup():
        import jax, jax.numpy as jnp
        import numpy as np
        D = 512
        H = 16
        HKV = 4
        HD = D // H
        REP = H // HKV
        DFF = 2048
        B, N = (4, 1024)
        EPS = 1e-05
        WSCALE = 0.02

        def _ln(x):
            m = jnp.mean(x, axis=-1, keepdims=True)
            v = jnp.mean(jnp.square(x - m), axis=-1, keepdims=True)
            return (x - m) * jax.lax.rsqrt(v + EPS)

        def _gqa_attn(h, wq, wk, wv, wo):
            b, n, d = h.shape
            q = (h @ wq.T).reshape(b, n, HKV, REP, HD)
            k = (h @ wk.T).reshape(b, n, HKV, HD)
            v = (h @ wv.T).reshape(b, n, HKV, HD)
            scores = jnp.einsum('bqgrh,bkgh->bgrqk', q, k) * (1.0 / np.sqrt(HD))
            a = jax.nn.softmax(scores, axis=-1)
            out = jnp.einsum('bgrqk,bkgh->bqgrh', a, v).reshape(b, n, d)
            return out @ wo.T

        def _mlp(h, w1, b1, w2, b2):
            h = jax.nn.gelu(h @ w1.T + b1, approximate=False)
            return h @ w2.T + b2
        key = jax.random.key(seed)
        ks = jax.random.split(key, 10)
        return {'x': jax.random.normal(ks[0], (B, N, D), jnp.float32), 'c': jax.random.normal(ks[1], (B, D), jnp.float32), 'wq': jax.random.normal(ks[2], (D, D), jnp.float32) * WSCALE, 'wk': jax.random.normal(ks[3], (HKV * HD, D), jnp.float32) * WSCALE, 'wv': jax.random.normal(ks[4], (HKV * HD, D), jnp.float32) * WSCALE, 'wo': jax.random.normal(ks[5], (D, D), jnp.float32) * WSCALE, 'w1': jax.random.normal(ks[6], (DFF, D), jnp.float32) * WSCALE, 'b1': jnp.zeros((DFF,), jnp.float32), 'w2': jax.random.normal(ks[7], (D, DFF), jnp.float32) * WSCALE, 'b2': jnp.zeros((D,), jnp.float32), 'wc': jax.random.normal(ks[8], (6 * D, D), jnp.float32) * WSCALE, 'bc': jnp.zeros((6 * D,), jnp.float32)}
    _L0_cond_all = _L0_cond_setup()
    _L0_cond_in = {k: v for k, v in _L0_cond_all.items() if k in ('wq', 'wk', 'wv', 'wo', 'w1', 'b1', 'w2', 'b2', 'wc', 'bc')}
    del _L0_cond_all
    return {'x': x, 'cond_1024': cond_1024, 'L0_cond_wq': _L0_cond_in['wq'], 'L0_cond_wk': _L0_cond_in['wk'], 'L0_cond_wv': _L0_cond_in['wv'], 'L0_cond_wo': _L0_cond_in['wo'], 'L0_cond_w1': _L0_cond_in['w1'], 'L0_cond_b1': _L0_cond_in['b1'], 'L0_cond_w2': _L0_cond_in['w2'], 'L0_cond_b2': _L0_cond_in['b2'], 'L0_cond_wc': _L0_cond_in['wc'], 'L0_cond_bc': _L0_cond_in['bc']}

def reference(x, cond_1024, L0_cond_wq, L0_cond_wk, L0_cond_wv, L0_cond_wo, L0_cond_w1, L0_cond_b1, L0_cond_w2, L0_cond_b2, L0_cond_wc, L0_cond_bc):
    import jax
    import jax.numpy as jnp

    def _L0_cond_ref(x, c, wq, wk, wv, wo, w1, b1, w2, b2, wc, bc):
        import jax, jax.numpy as jnp
        import numpy as np
        D = 512
        H = 16
        HKV = 4
        HD = D // H
        REP = H // HKV
        DFF = 2048
        B, N = (4, 1024)
        EPS = 1e-05
        WSCALE = 0.02

        def _ln(x):
            m = jnp.mean(x, axis=-1, keepdims=True)
            v = jnp.mean(jnp.square(x - m), axis=-1, keepdims=True)
            return (x - m) * jax.lax.rsqrt(v + EPS)

        def _gqa_attn(h, wq, wk, wv, wo):
            b, n, d = h.shape
            q = (h @ wq.T).reshape(b, n, HKV, REP, HD)
            k = (h @ wk.T).reshape(b, n, HKV, HD)
            v = (h @ wv.T).reshape(b, n, HKV, HD)
            scores = jnp.einsum('bqgrh,bkgh->bgrqk', q, k) * (1.0 / np.sqrt(HD))
            a = jax.nn.softmax(scores, axis=-1)
            out = jnp.einsum('bgrqk,bkgh->bqgrh', a, v).reshape(b, n, d)
            return out @ wo.T

        def _mlp(h, w1, b1, w2, b2):
            h = jax.nn.gelu(h @ w1.T + b1, approximate=False)
            return h @ w2.T + b2
        cond = jax.nn.silu(c) @ wc.T + bc
        sh1, sc1, g1, sh2, sc2, g2 = jnp.split(cond, 6, axis=-1)
        sh1, sc1, g1 = (sh1[:, None], sc1[:, None], g1[:, None])
        sh2, sc2, g2 = (sh2[:, None], sc2[:, None], g2[:, None])
        h = _ln(x) * (1.0 + sc1) + sh1
        x = x + g1 * _gqa_attn(h, wq, wk, wv, wo)
        h = _ln(x) * (1.0 + sc2) + sh2
        x = x + g2 * _mlp(h, w1, b1, w2, b2)
        return x
    x = _L0_cond_ref(x, cond_1024, L0_cond_wq, L0_cond_wk, L0_cond_wv, L0_cond_wo, L0_cond_w1, L0_cond_b1, L0_cond_w2, L0_cond_b2, L0_cond_wc, L0_cond_bc)
    return x

_drawn_inputs = setup_inputs


def setup_inputs(seed=0):
    import zlib

    import numpy as np

    out = dict(_drawn_inputs(seed))
    spreads = {'L0_cond_b1': (0.0, 0.542), 'L0_cond_b2': (0.0, 0.31), 'L0_cond_bc': (0.0, 0.1)}
    factors = {'L0_cond_wq': 8.0, 'L0_cond_wk': 8.0, 'L0_cond_wv': 2.97, 'L0_cond_wo': 3.152}
    for name, (base, spread) in spreads.items():
        noise = np.random.default_rng([zlib.crc32(name.encode()), seed]).standard_normal(out[name].shape)
        drawn = base * np.exp(spread * noise) if base else spread * noise
        out[name] = jnp.asarray(drawn.astype(out[name].dtype))
    for name, factor in factors.items():
        out[name] = (out[name] * factor).astype(out[name].dtype)
    return out
```

```python
import concourse.bass as bass
from concourse import mybir
from contextlib import ExitStack


P = 128
B, N, D = 8, 512, 512
HKV, R, HD = 4, 4, 32
DFF = 2048
TT = N // P
KD = D // P
NJ = DFF // P
NC = 6 * KD
SH1, SC1, G1, SH2, SC2, G2 = (i * KD for i in range(6))
EPS = 1e-5
SCORE_SCALE = 1.0 / float(HD) ** 0.5
STACK = 3 * HD
STACKED = 3 * R * 16
SHIFT = STACK + 2

SCORES = [[f"S{g}_{i}" for i in range(R * TT)] for g in range(HKV)]
UNITS_FIRST = (["T0", "T1", "T2", "T3", "K", "Q0", "Q1", "Q2", "Q3", "V", "VT"] + SCORES[0] + ["M0"])
FILL = {(0, 3): ["T0", "T1", "T2", "T3"], (1, 3): ["K"], (2, 3): ["Q0"], (3, 1): ["Q1"], (3, 3): ["Q2"]}
TAIL = (["Q3"] + SCORES[0][0:4] + ["V", "VT"] + SCORES[0][4:12] + ["O0"] + SCORES[0][12:16]
        + ["O1", "M0", "O2", "O3"])


def unit_order(has_next):
    order = []
    for g in range(HKV):
        for kt in range(TT):
            if g + 1 < HKV:
                order += SCORES[g + 1][4 * kt:4 * kt + 4]
                if kt == TT - 1:
                    order += [f"M{g + 1}"]
            if has_next:
                order += FILL.get((g, kt), [])
    return order + (TAIL if has_next else ["O0", "O1", "O2", "O3"])


AT_FIRST = {name: i for i, name in enumerate(UNITS_FIRST)}
AT_FULL = {name: i for i, name in enumerate(unit_order(True))}
AT_LAST = {name: i for i, name in enumerate(unit_order(False))}
PER_SEQ = len(AT_FULL)


class Units:

    def __init__(self, at, base):
        self.at, self.base = at, base

    def bank(self, name):
        return self.at[name] % 2

    def done(self, name):
        return self.base + (self.at[name] + 1)

    def before(self, name):
        return self.base + self.at[name]

    def room(self, name):
        return self.base + max(self.at[name] - 1, 0)


def first_units():
    return Units(AT_FIRST, 0)


def seq_units(b, has_next=True):
    return Units(AT_FULL if has_next else AT_LAST, len(UNITS_FIRST) + b * PER_SEQ)


def layer_kernel(nc, x, cond, wq, wk, wv, wo, w1, b1, w2, b2, wc, bc, out):
    f32, f32r = mybir.dt.float32, mybir.dt.float32r
    ALU, ACT, AX = mybir.AluOpType, mybir.ActivationFunctionType, mybir.AxisListType

    x1_dram = nc.dram_tensor("x1_scratch", (B, N, D), f32, kind="Internal").ap()
    gate_dram = nc.dram_tensor("gate_scratch", (B, 2, D), f32, kind="Internal").ap()

    def seq_dram(t, b):
        return t[bass.ds(b, 1), :, :].rearrange("a (t p) d -> p (a t) d", p=P)

    def as_f32(ap):
        return ap.bitcast(f32)

    with ExitStack() as ctx:
        def sb(stack, name, shape, dt=f32):
            return stack.enter_context(nc.sbuf_tensor(name, shape, dt))

        def ps(stack, name, shape, dt=f32):
            return stack.enter_context(nc.psum_tensor(name, shape, dt))

        def sem(name):
            return ctx.enter_context(nc.semaphore(name))

        ident = sb(ctx, "ident", [P, P])
        cond_cols = sb(ctx, "cond_cols", [P, B, NC])
        bias_cols = sb(ctx, "bias_cols", [P, NC + NJ])
        neg_half = sb(ctx, "neg_half", [P, TT])

        attn_ctx = ExitStack()
        with attn_ctx:
            wq_t = [sb(attn_ctx, f"wq_t{i}", [P, KD, D], f32r) for i in range(2)]
            wk_t = [sb(attn_ctx, f"wk_t{i}", [P, KD, P], f32r) for i in range(2)]
            wv_t = [sb(attn_ctx, f"wv_t{i}", [P, KD, P], f32r) for i in range(2)]
            wo_t = [sb(attn_ctx, f"wo_t{i}", [P, KD, D], f32r) for i in range(2)]

            prologue(nc, f32, f32r, ALU, ACT, sb, ps, sem, ident, cond_cols, bias_cols, neg_half,
                     wq_t, wk_t, wv_t, wo_t, cond, wq, wk, wv, wo, b1, wc, bc, gate_dram)
            attention(nc, f32, f32r, ALU, ACT, AX, sb, ps, sem, as_f32, seq_dram, ident, cond_cols, neg_half,
                      wq_t, wk_t, wv_t, wo_t, x, x1_dram, gate_dram)
        mlp(nc, f32, f32r, ALU, ACT, sb, ps, sem, as_f32, seq_dram, ident, cond_cols, bias_cols, neg_half,
            w1, w2, b2, x1_dram, gate_dram, out)


def prologue(nc, f32, f32r, ALU, ACT, sb, ps, sem, ident, cond_cols, bias_cols, neg_half,
             wq_t, wk_t, wv_t, wo_t, cond, wq, wk, wv, wo, b1, wc, bc, gate_dram):
    with ExitStack() as st:
        c_row = sb(st, "c_row", [B, D])
        silu_row = sb(st, "silu_row", [B, D])
        silu_t = sb(st, "silu_t", [P, KD, B])
        bias_rows = sb(st, "bias_rows", [NC + NJ, P])
        wc_in = sb(st, "wc_in", [P, NC, D])
        wc_turned = [sb(st, f"wc_turned{i}", [P, KD, P]) for i in range(4)]
        gate_rows = sb(st, "gate_rows", [B, 2, D])
        attn_in = {"q": sb(st, "wq_in", [P, KD, D]), "k": sb(st, "wk_in", [P, 1, D]),
                   "v": sb(st, "wv_in", [P, 1, D]), "o": sb(st, "wo_in", [P, KD, D])}
        wc_bank = [ps(st, f"wc_bank{i}", [P, D]) for i in range(4)]
        cond_bank = ps(st, "cond_bank", [P, NC, B])
        small_bank = ps(st, "small_bank", [P, D])
        w_bank = [ps(st, f"w_bank{i}", [P, D]) for i in range(2)]

        ident_zero, ident_ready = sem("ident_zero"), sem("ident_ready")
        c_loaded, bias_loaded = sem("c_loaded"), sem("bias_loaded")
        wc_loaded = [sem(f"wc_loaded{i}") for i in range(6)]
        w_loaded = {n: sem(f"w{n}_loaded") for n in "qkvo"}
        silu_done, silu_turned, silu_taken = sem("silu_done"), sem("silu_turned"), sem("silu_taken")
        bias_turned, bias_taken = sem("bias_turned"), sem("bias_taken")
        w_turned, w_hi, w_split = sem("w_turned"), sem("w_hi"), sem("w_split")
        wc_done = sem("wc_done")
        wc_taken = [sem("wc_taken_act"), sem("wc_taken_dve")]
        cond_done, cond_ready = sem("cond_done"), sem("cond_ready")
        gates_turned, gates_taken, gates_stored = sem("gates_turned"), sem("gates_taken"), sem("gates_stored")

        w_units = [("q", kt) for kt in range(KD)] + [("k", 0), ("v", 0)] + [("o", kt) for kt in range(KD)]
        w_dst = {"q": wq_t, "k": wk_t, "v": wv_t, "o": wo_t}

        def unit_dst(u, half):
            which, kt = w_units[u]
            return w_dst[which][half][:, kt, :] if which in "qo" else w_dst[which][half][:, :, :].rearrange("p k n -> p (k n)")

        with nc.Block() as block:
            @block.sync
            def _(sp):
                sp.dma_start(c_row[:, :], cond).then_inc(c_loaded, 16)
                sp.dma_start(bias_rows[0:NC, :], bc.rearrange("(j p) -> j p", p=P)).then_inc(bias_loaded, 16)
                sp.dma_start(bias_rows[NC:NC + NJ, :], b1.rearrange("(j p) -> j p", p=P)).then_inc(bias_loaded, 16)
                for n, w in (("q", wq), ("k", wk), ("v", wv), ("o", wo)):
                    sp.dma_start(attn_in[n][:, :, :], w.rearrange("(o p) i -> p o i", p=P)).then_inc(w_loaded[n], 16)
                for i in range(6):
                    sp.dma_start(wc_in[:, KD * i:KD * i + KD, :],
                                 wc[D * i:D * i + D, :].rearrange("(o p) i -> p o i", p=P)).then_inc(wc_loaded[i], 16)
                sp.wait_ge(gates_taken, 2)
                sp.dma_start(gate_dram, gate_rows[:, :, :]).then_inc(gates_stored, 16)
                sp.wait_ge(gates_stored, 16)

            @block.gpsimd
            def _(pool):
                nc.gpsimd.memset(ident[:, :], 0.0).then_inc(ident_zero, 1)
                pool.wait_ge(ident_zero, 1)
                nc.gpsimd.affine_select(out=ident[:, :], in_=ident[:, :], compare_op=ALU.not_equal, fill=1.0,
                                        base=0, pattern=[[-1, P]], channel_multiplier=1).then_inc(ident_ready, 1)
                nc.gpsimd.memset(neg_half[:, :], -0.5).then_inc(ident_zero, 1)

            @block.scalar
            def _(act):
                act.wait_ge(c_loaded, 16)
                nc.scalar.activation(silu_row[:, :], c_row[:, :], ACT.Silu).then_inc(silu_done, 1)
                for u in range(len(w_units)):
                    act.wait_ge(w_turned, u + 1)
                    nc.scalar.activation(unit_dst(u, 0), w_bank[u % 2][:, :], ACT.Copy).then_inc(w_hi, 1)
                for j in range(0, NC, 2):
                    act.wait_ge(wc_done, j + 1)
                    if j >= 4:
                        act.wait_ge(cond_done, j - 3)
                    nc.scalar.activation(wc_turned[j % 4][:, :, :].rearrange("p k n -> p (k n)"), wc_bank[j % 4][:, :],
                                         ACT.Copy).then_inc(wc_taken[0], 1)

            @block.vector
            def _(dve):
                dve.wait_ge(silu_turned, 1)
                nc.vector.tensor_copy(silu_t[:, :, :].rearrange("p k b -> p (k b)"),
                                      small_bank[:, 0:KD * B]).then_inc(silu_taken, 1)
                dve.wait_ge(bias_turned, 1)
                nc.vector.tensor_copy(bias_cols[:, :], small_bank[:, 0:NC + NJ]).then_inc(bias_taken, 1)
                for u in range(len(w_units)):
                    dve.wait_ge(w_hi, u + 1)
                    nc.vector.tensor_tensor(unit_dst(u, 1), w_bank[u % 2][:, :], unit_dst(u, 0).bitcast(f32),
                                            ALU.subtract).then_inc(w_split, 1)
                for j in range(1, NC, 2):
                    dve.wait_ge(wc_done, j + 1)
                    if j >= 4:
                        dve.wait_ge(cond_done, j - 3)
                    nc.vector.tensor_copy(wc_turned[j % 4][:, :, :].rearrange("p k n -> p (k n)"),
                                          wc_bank[j % 4][:, :]).then_inc(wc_taken[1], 1)
                dve.wait_ge(cond_done, NC)
                dve.wait_ge(bias_taken, 1)
                for j in range(NC):
                    one = 1.0 if j // KD in (1, 4) else 0.0
                    nc.vector.tensor_scalar(cond_cols[:, :, j], cond_bank[:, j, :], bias_cols[:, j:j + 1], one,
                                            ALU.add, ALU.add).then_inc(cond_ready, 1)
                for i in range(2):
                    dve.wait_ge(gates_turned, i + 1)
                    nc.vector.tensor_copy(gate_rows[:, i, :], w_bank[i][0:B, :]).then_inc(gates_taken, 1)

            @block.tensor
            def _(pe):
                pe.wait_ge(ident_ready, 1)
                pe.wait_ge(silu_done, 1)
                for kt in range(KD):
                    last = nc.tensor.transpose(small_bank[:, kt * B:kt * B + B], silu_row[:, kt * P:kt * P + P],
                                               ident[0:B, 0:B])
                last.then_inc(silu_turned, 1)
                pe.wait_ge(silu_taken, 1)
                pe.wait_ge(bias_loaded, 32)
                nc.tensor.transpose(small_bank[:, 0:NC + NJ], bias_rows[:, :],
                                    ident[0:NC + NJ, 0:NC + NJ]).then_inc(bias_turned, 1)
                for u, (which, kt) in enumerate(w_units):
                    pe.wait_ge(w_loaded[which], 16)
                    if u >= 2:
                        pe.wait_ge(w_split, u - 1)
                    for i in range(KD):
                        src = (attn_in[which][:, i, kt * P:kt * P + P] if which in "qo"
                               else attn_in[which][:, 0, i * P:i * P + P])
                        last = nc.tensor.transpose(w_bank[u % 2][:, i * P:i * P + P], src, ident[:, :])
                    last.then_inc(w_turned, 1)
                for j in range(NC + 1):
                    if j < NC:
                        pe.wait_ge(wc_loaded[j // KD], 16)
                        if j >= 4:
                            pe.wait_ge(wc_taken[j % 2], j // 2 - 1)
                        for kt in range(KD):
                            last = nc.tensor.transpose(wc_bank[j % 4][:, kt * P:kt * P + P],
                                                       wc_in[:, j, kt * P:kt * P + P], ident[:, :])
                        last.then_inc(wc_done, 1)
                    if j >= 1:
                        i = j - 1
                        pe.wait_ge(wc_taken[i % 2], i // 2 + 1)
                        for kt in range(KD):
                            last = nc.tensor.matmul(cond_bank[:, i, :], wc_turned[i % 4][:, kt, :], silu_t[:, kt, :],
                                                    start=(kt == 0), stop=(kt == KD - 1))
                        last.then_inc(cond_done, 1)
                pe.wait_ge(cond_ready, NC)
                pe.wait_ge(w_split, len(w_units))
                for i, j0 in enumerate((G1, G2)):
                    for kt in range(KD):
                        last = nc.tensor.transpose(w_bank[i][0:B, kt * P:kt * P + P], cond_cols[:, :, j0 + kt],
                                                   ident[:, :])
                    last.then_inc(gates_turned, 1)


def attention(nc, f32, f32r, ALU, ACT, AX, sb, ps, sem, as_f32, seq_dram, ident, cond_cols, neg_half,
              wq_t, wk_t, wv_t, wo_t, x, x1_dram, gate_dram):
    with ExitStack() as st:
        xa = sb(st, "xa", [P, TT, D])
        stats = sb(st, "stats", [P, TT, 6])
        mean_var = sb(st, "mean_var", [P, TT, 2])
        var_eps = sb(st, "var_eps", [P, TT])
        rstd = sb(st, "rstd", [P, TT])
        shift_col = sb(st, "shift_col", [P, TT])
        cond_now = sb(st, "cond_now", [P, NC])
        h_full = [sb(st, f"h_full{i}", [P, N]) for i in range(2)]
        h = [sb(st, f"h{i}", [P, KD, N], f32r) for i in range(2)]
        k_part = [sb(st, f"k_part{i}", [P, N], f32r) for i in range(2)]
        q_part = [[sb(st, f"q_part{s}{i}", [P, N], f32r) for i in range(2)] for s in range(2)]
        v_full = sb(st, "v_full", [P, N])
        v = sb(st, "v", [P, TT, P])
        k_stack = sb(st, "k_stack", [P, HKV, N], f32r)
        q_stack = sb(st, "q_stack", [P, HKV, R, N], f32r)
        neg_max = sb(st, "neg_max", [P, 2, R * TT])
        max_row = [sb(st, f"max_row{i}", [R * TT, P], f32r) for i in range(2)]
        probs = [sb(st, f"probs{i}", [P, R, N]) for i in range(TT)]
        probs_sum = sb(st, "probs_sum", [P, R, N])
        ones = sb(st, "ones", [P, HD])
        inv_sum = sb(st, "inv_sum", [P, N])
        attn_raw = sb(st, "attn_raw", [P, N])
        attn_full = sb(st, "attn_full", [P, N])
        attn = [sb(st, f"attn{i}", [P, HKV, N], f32r) for i in range(2)]
        gated = [sb(st, f"gated{i}", [P, D]) for i in range(2)]
        resid = sb(st, "resid", [P, TT, D])
        gate_now = sb(st, "gate_now", [P, D])

        pair = [ps(st, f"pair{i}", [P, 2, N]) for i in range(2)]
        pv_bank = ps(st, "pv_bank", [P, N])
        sum_bank = ps(st, "sum_bank", [P, N])
        work = [ps(st, f"work{i}", [P, N]) for i in range(2)]

        unit_ready, unit_taken = sem("unit_ready"), sem("unit_taken")
        consts_ready = sem("consts_ready")
        x_loaded, stats_done, moments_done, eps_added = sem("x_loaded"), sem("stats_done"), sem("moments_done"), sem("eps_added")
        rstd_ready, shift_ready, normed, cond_copied = sem("rstd_ready"), sem("shift_ready"), sem("normed"), sem("cond_copied")
        h_ready, h_hi, h_split = sem("h_ready"), sem("h_hi"), sem("h_split")
        k_hi, q_hi, v_taken = sem("k_hi"), sem("q_hi"), sem("v_taken")
        k_stacked, q_stacked = sem("k_stacked"), [sem(f"q_stacked{i}") for i in range(2)]
        max_hi, max_stacked = sem("max_hi"), sem("max_stacked")
        pair_ready, exp_done, pv_done, pv_copied = sem("pair_ready"), sem("exp_done"), sem("pv_done"), sem("pv_copied")
        added, sums_ready, sums_taken = sem("added"), sem("sums_ready"), sem("sums_taken")
        attn_scaled, attn_hi, attn_split = sem("attn_scaled"), sem("attn_hi"), sem("attn_split")
        gate_loaded, resid_loaded, x1_added, x1_stored = sem("gate_loaded"), sem("resid_loaded"), sem("x1_added"), sem("x1_stored")

        def group_no(b, g):
            return b * HKV + g

        def stacked(b, g):
            return b * (HKV // 2 * STACKED) + (g // 2 + 1) * STACKED

        def tile_no(b, g, kt):
            return b * (HKV * TT) + (g * TT + kt)

        def sequences(eng, first, middle, last):
            first()
            middle(0, True)
            with eng.Fori(1, B - 1) as b:
                middle(b, False)
            last(B - 1)

        with nc.Block() as block:
            @block.sync
            def _(sp):
                def load_x(b, u, first=False):
                    if not first:
                        sp.wait_ge(unit_ready, u)
                    sp.dma_start(xa[:, :, :], seq_dram(x, b)).then_inc(x_loaded, 16)

                def load_resid(b):
                    sp.dma_start(gate_now[:, :], gate_dram[bass.ds(b, 1), 0, :].partition_broadcast(P).rearrange("p a d -> p (a d)")).then_inc(gate_loaded, 16)
                    sp.dma_start(resid[:, :, :], seq_dram(x, b)).then_inc(resid_loaded, 16)

                def store_x1(b):
                    sp.wait_ge(x1_added, b * TT + TT)
                    sp.dma_start(seq_dram(x1_dram, b), resid[:, :, :]).then_inc(x1_stored, 16)
                    sp.wait_ge(x1_stored, b * 16 + 16)

                def stack_k():
                    for g in range(HKV):
                        for row, part in ((0, 0), (1, 0), (2, 1)):
                            sp.dma_start(as_f32(k_stack[HD * row:HD * row + HD, g, :]),
                                         as_f32(k_part[part][HD * g:HD * g + HD, :])).then_inc(k_stacked, 16)

                def stack_q(u, g):
                    sp.wait_ge(unit_taken, u.done(f"Q{g}"))
                    for r in range(R):
                        for row, part in ((0, 0), (1, 1), (2, 0)):
                            sp.dma_start(as_f32(q_stack[HD * row:HD * row + HD, g, r, :]),
                                         as_f32(q_part[g % 2][part][HD * r:HD * r + HD, :])).then_inc(q_stacked[g % 2], 16)

                def stack_max(u, g):
                    sp.wait_ge(unit_taken, u.done(f"M{g}"))
                    for part in range(2):
                        row = as_f32(q_stack[STACK + part:STACK + part + 1, g, :, :])
                        sp.dma_start(row.rearrange("o r n -> o (r n)"),
                                     as_f32(max_row[part][:, :])).then_inc(max_stacked, 16)

                def first():
                    u = first_units()
                    load_x(0, None, first=True)
                    sp.wait_ge(unit_taken, u.done("K"))
                    stack_k()
                    for g in range(HKV):
                        stack_q(u, g)
                    stack_max(u, 0)

                def sequence(b, is_first, has_next=True):
                    u = seq_units(b, has_next)
                    if has_next:
                        load_x(b + 1, AT_FIRST["T3"] + 1 if is_first else u.base - PER_SEQ + (AT_FULL["T3"] + 1))
                    if not is_first:
                        store_x1(b - 1)
                    load_resid(b)
                    for g in range(1, HKV):
                        stack_max(u, g)
                    if has_next:
                        stack_q(u, 0)
                        stack_q(u, 1)
                        sp.wait_ge(pair_ready, tile_no(b, HKV - 1, TT - 1) * 2 + 2)
                        stack_k()
                        stack_q(u, 2)
                        stack_q(u, 3)
                        stack_max(u, 0)
                    else:
                        store_x1(b)

                sequences(sp, first, sequence, lambda b: sequence(b, False, has_next=False))

            @block.gpsimd
            def _(pool):
                def rstd_of(b):
                    pool.wait_ge(eps_added, b + 1)
                    nc.gpsimd.tensor_tensor(rstd[:, :], var_eps[:, :], neg_half[:, :], ALU.pow).then_inc(rstd_ready, 1)

                def first():
                    nc.gpsimd.memset(as_f32(k_stack[STACK:SHIFT, :, :]), 1.0).then_inc(consts_ready, 1)
                    pool.wait_ge(consts_ready, 1)
                    nc.gpsimd.memset(ones[:, :], 1.0).then_inc(consts_ready, 1)
                    rstd_of(0)

                def sequence(b, is_first, has_next=True):
                    u = seq_units(b, has_next)
                    if has_next:
                        rstd_of(b + 1)
                    for g in range(HKV):
                        if not (is_first and g == 0):
                            pool.wait_ge(sums_ready, group_no(b, g))
                        for kt in range(1, TT):
                            pool.wait_ge(exp_done, tile_no(b, g, kt) * 2 + 2)
                            if kt > 1:
                                pool.wait_ge(added, group_no(b, g) * (TT - 1) + (kt - 1))
                            first_in = probs[0] if kt == 1 else probs_sum
                            nc.gpsimd.tensor_tensor(probs_sum[:, :, :], first_in[:, :, :], probs[kt][:, :, :],
                                                    ALU.add).then_inc(added, 1)
                    pool.wait_ge(resid_loaded, b * 16 + 16)
                    for tt in range(TT):
                        pool.wait_ge(unit_taken, u.done(f"O{tt}"))
                        nc.gpsimd.tensor_tensor(resid[:, tt, :], resid[:, tt, :], gated[tt % 2][:, :],
                                                ALU.add).then_inc(x1_added, 1)

                sequences(pool, first, sequence, lambda b: sequence(b, False, has_next=False))

            @block.scalar
            def _(act):
                def norm(b):
                    act.wait_ge(shift_ready, b + 1)
                    for tt in range(TT):
                        nc.scalar.activation(xa[:, tt, :], xa[:, tt, :], ACT.Identity, scale=rstd[:, tt:tt + 1],
                                             bias=shift_col[:, tt:tt + 1]).then_inc(normed, 1)

                def modulate(b, u, is_first=False):
                    act.wait_ge(cond_copied, b + 1)
                    for kt in range(KD):
                        act.wait_ge(unit_ready, u.done(f"T{kt}"))
                        if not (is_first and kt < 2):
                            act.wait_ge(h_split, b * KD + (kt - 1))
                        nc.scalar.activation(h_full[kt % 2][:, :], work[u.bank(f"T{kt}")][:, :], ACT.Identity,
                                             scale=cond_now[:, SC1 + kt:SC1 + kt + 1],
                                             bias=cond_now[:, SH1 + kt:SH1 + kt + 1]).then_inc(h_ready, 1)

                def k_high(b, u, is_first=False):
                    act.wait_ge(unit_ready, u.done("K"))
                    if not is_first:
                        act.wait_ge(k_stacked, b * STACKED)
                    nc.scalar.activation(k_part[0][:, :], work[u.bank("K")][:, :], ACT.Copy).then_inc(k_hi, 1)

                def q_high(b, g, u, is_first=False):
                    act.wait_ge(unit_ready, u.done(f"Q{g}"))
                    if not (is_first and g < 2):
                        act.wait_ge(q_stacked[g % 2], stacked(b, g) - STACKED)
                    nc.scalar.activation(q_part[g % 2][0][:, :], work[u.bank(f"Q{g}")][:, :], ACT.Copy,
                                         scale=SCORE_SCALE).then_inc(q_hi, 1)

                def max_high(b, g, u, is_first=False):
                    act.wait_ge(unit_ready, u.done(f"M{g}"))
                    if not is_first:
                        act.wait_ge(max_stacked, group_no(b, g) * 32)
                    nc.scalar.activation(max_row[0][:, :], work[u.bank(f"M{g}")][0:R * TT, 0:P], ACT.Copy).then_inc(max_hi, 1)

                def exps(b, g, kt, is_first):
                    t = tile_no(b, g, kt)
                    if not (is_first and g == 0):
                        act.wait_ge(pv_done, t - (TT - 1))
                        act.wait_ge(added, group_no(b, g) * (TT - 1) - (TT - 1) + max(kt, 1))
                    for p in range(2):
                        act.wait_ge(pair_ready, t * 2 + (p + 1))
                        nc.scalar.activation(probs[kt][:, 2 * p:2 * p + 2, :], pair[p][:, :, :], ACT.Exp).then_inc(exp_done, 1)

                def copy_pv(b, g, is_first):
                    act.wait_ge(pv_done, tile_no(b, g, TT - 1) + 1)
                    if not (is_first and g == 0):
                        act.wait_ge(attn_scaled, group_no(b, g))
                    nc.scalar.activation(attn_raw[:, :], pv_bank[:, :], ACT.Copy).then_inc(pv_copied, 1)

                def first():
                    u = first_units()
                    norm(0)
                    modulate(0, u, is_first=True)
                    k_high(0, u, is_first=True)
                    for g in range(HKV):
                        q_high(0, g, u, is_first=True)
                    max_high(0, 0, u, is_first=True)

                def sequence(b, is_first, has_next=True):
                    u = seq_units(b, has_next)
                    for g in range(HKV):
                        for kt in range(TT):
                            if kt == 0 and g > 0:
                                copy_pv(b, g - 1, is_first)
                            exps(b, g, kt, is_first)
                            if kt == TT - 1 and g + 1 < HKV:
                                max_high(b, g + 1, u)
                            if has_next:
                                if (g, kt) == (0, 2):
                                    norm(b + 1)
                                for name in FILL.get((g, kt), []):
                                    if name == "T0":
                                        modulate(b + 1, u)
                                    elif name == "K":
                                        k_high(b + 1, u)
                                    elif name[0] == "Q":
                                        q_high(b + 1, int(name[1]), u)
                    copy_pv(b, HKV - 1, is_first)
                    if has_next:
                        q_high(b + 1, 3, u)
                        max_high(b + 1, 0, u)

                sequences(act, first, sequence, lambda b: sequence(b, False, has_next=False))

            @block.vector
            def _(dve):
                def copy_cond(b):
                    nc.vector.tensor_copy(cond_now[:, :], cond_cols[:, bass.ds(b, 1), :].rearrange("p a j -> p (a j)")).then_inc(cond_copied, 1)

                def tile_stats():
                    for tt in range(TT):
                        nc.vector.bn_stats(stats[:, tt, :], xa[:, tt, :]).then_inc(stats_done, 1)

                def moments(b):
                    for tt in range(TT):
                        nc.vector.bn_aggr(mean_var[:, tt, :], stats[:, tt, :]).then_inc(moments_done, 1)
                    dve.wait_ge(moments_done, b * TT + TT)
                    nc.vector.tensor_scalar(var_eps[:, :], mean_var[:, :, 1], EPS, None, ALU.add).then_inc(eps_added, 1)

                def shift_of(b):
                    dve.wait_ge(rstd_ready, b + 1)
                    nc.vector.scalar_tensor_tensor(out=shift_col[:, :], in0=mean_var[:, :, 0], scalar=-1.0,
                                                   in1=rstd[:, :], op0=ALU.mult, op1=ALU.mult).then_inc(shift_ready, 1)

                def split_h(b, u):
                    for kt in range(KD):
                        dve.wait_ge(h_ready, b * KD + (kt + 1))
                        nc.vector.tensor_copy(h[0][:, kt, :], h_full[kt % 2][:, :]).then_inc(unit_taken, 1)
                        dve.wait_ge(unit_taken, u.done(f"T{kt}"))
                        nc.vector.tensor_tensor(h[1][:, kt, :], h_full[kt % 2][:, :], as_f32(h[0][:, kt, :]),
                                                ALU.subtract).then_inc(h_split, 1)

                def k_low(b, u):
                    dve.wait_ge(k_hi, b + 1)
                    nc.vector.tensor_tensor(k_part[1][:, :], work[u.bank("K")][:, :], as_f32(k_part[0][:, :]),
                                            ALU.subtract).then_inc(unit_taken, 1)

                def q_low(b, g, u):
                    dve.wait_ge(q_hi, group_no(b, g) + 1)
                    nc.vector.scalar_tensor_tensor(out=q_part[g % 2][1][:, :], in0=work[u.bank(f"Q{g}")][:, :],
                                                   scalar=SCORE_SCALE, in1=as_f32(q_part[g % 2][0][:, :]),
                                                   op0=ALU.mult, op1=ALU.subtract).then_inc(unit_taken, 1)

                def take_v(b, u):
                    dve.wait_ge(unit_ready, u.done("V"))
                    nc.vector.tensor_copy(v_full[:, :], work[u.bank("V")][:, :]).then_inc(unit_taken, 1)

                def take_vt(b, u, is_first=False):
                    dve.wait_ge(unit_ready, u.done("VT"))
                    if not is_first:
                        dve.wait_ge(pv_done, b * (HKV * TT))
                    nc.vector.tensor_copy(v[:, :, :].rearrange("p t n -> p (t n)"),
                                          work[u.bank("VT")][:, :]).then_inc(unit_taken, 1)

                def row_max(b, g, i, u):
                    name = f"S{g}_{i}"
                    dve.wait_ge(unit_ready, u.done(name))
                    nc.vector.tensor_reduce(out=neg_max[:, g % 2, i:i + 1], in_=work[u.bank(name)][:, :], op=ALU.max,
                                            axis=AX.X, negate=True).then_inc(unit_taken, 1)

                def max_low(b, g, u):
                    dve.wait_ge(max_hi, group_no(b, g) + 1)
                    nc.vector.tensor_tensor(max_row[1][:, :], work[u.bank(f"M{g}")][0:R * TT, 0:P],
                                            as_f32(max_row[0][:, :]), ALU.subtract).then_inc(unit_taken, 1)

                def invert(b, g, c):
                    if c == 0:
                        dve.wait_ge(sums_ready, group_no(b, g) + 1)
                    ins = nc.vector.reciprocal(inv_sum[:, c * P:c * P + P], sum_bank[:, c * P:c * P + P])
                    if c == TT - 1:
                        ins.then_inc(sums_taken, 1)

                def finish_group(b, g):
                    n = group_no(b, g) + 1
                    dve.wait_ge(sums_taken, n)
                    dve.wait_ge(pv_copied, n)
                    nc.vector.tensor_tensor(attn_full[:, :], attn_raw[:, :], inv_sum[:, :], ALU.mult).then_inc(attn_scaled, 1)
                    dve.wait_ge(attn_scaled, n)
                    nc.vector.tensor_copy(attn[0][:, g, :], attn_full[:, :]).then_inc(attn_hi, 1)
                    dve.wait_ge(attn_hi, n)
                    nc.vector.tensor_tensor(attn[1][:, g, :], attn_full[:, :], as_f32(attn[0][:, g, :]),
                                            ALU.subtract).then_inc(attn_split, 1)

                def gate(b, tt, u, is_first):
                    name = f"O{tt}"
                    dve.wait_ge(unit_ready, u.done(name))
                    if tt == 0:
                        dve.wait_ge(gate_loaded, b * 16 + 16)
                    if not (is_first and tt < 2):
                        dve.wait_ge(x1_added, b * TT + (tt - 1))
                    nc.vector.tensor_tensor(gated[tt % 2][:, :], work[u.bank(name)][:, :], gate_now[:, :],
                                            ALU.mult).then_inc(unit_taken, 1)

                def first():
                    u = first_units()
                    copy_cond(0)
                    dve.wait_ge(x_loaded, 16)
                    tile_stats()
                    dve.wait_ge(stats_done, TT)
                    moments(0)
                    shift_of(0)
                    split_h(0, u)
                    k_low(0, u)
                    for g in range(HKV):
                        q_low(0, g, u)
                    take_v(0, u)
                    take_vt(0, u, is_first=True)
                    for i in range(R * TT):
                        row_max(0, 0, i, u)
                    max_low(0, 0, u)

                def sequence(b, is_first, has_next=True):
                    u = seq_units(b, has_next)
                    for g in range(HKV):
                        for kt in range(TT):
                            if has_next and (g, kt) == (0, 0):
                                copy_cond(b + 1)
                                dve.wait_ge(x_loaded, b * 16 + 32)
                                tile_stats()
                            if has_next and (g, kt) == (0, 1):
                                dve.wait_ge(stats_done, b * TT + 2 * TT)
                            for i in range(R):
                                if g + 1 < HKV:
                                    row_max(b, g + 1, R * kt + i, u)
                                if kt == 2 and g > 0:
                                    invert(b, g - 1, i)
                            if kt == TT - 1 and g + 1 < HKV:
                                max_low(b, g + 1, u)
                            if has_next:
                                if (g, kt) == (0, 1):
                                    moments(b + 1)
                                if (g, kt) == (0, 2):
                                    shift_of(b + 1)
                                for name in FILL.get((g, kt), []):
                                    if name == "T0":
                                        split_h(b + 1, u)
                                    elif name == "K":
                                        k_low(b + 1, u)
                                    elif name[0] == "Q":
                                        q_low(b + 1, int(name[1]), u)
                            if kt == TT - 1 and g > 0:
                                finish_group(b, g - 1)
                    if has_next:
                        q_low(b + 1, 3, u)
                        for i in range(4):
                            row_max(b + 1, 0, i, u)
                        take_v(b + 1, u)
                        take_vt(b + 1, u)
                    for i in range(4):
                        if has_next:
                            row_max(b + 1, 0, 4 + i, u)
                        invert(b, HKV - 1, i)
                    finish_group(b, HKV - 1)
                    if has_next:
                        for i in range(8, 12):
                            row_max(b + 1, 0, i, u)
                    gate(b, 0, u, is_first)
                    if has_next:
                        for i in range(12, 16):
                            row_max(b + 1, 0, i, u)
                    gate(b, 1, u, is_first)
                    if has_next:
                        max_low(b + 1, 0, u)
                    gate(b, 2, u, is_first)
                    gate(b, 3, u, is_first)

                sequences(dve, first, sequence, lambda b: sequence(b, False, has_next=False))

            @block.tensor
            def _(pe):
                def room(u, name):
                    if u.at is not AT_FIRST or u.at[name] > 1:
                        pe.wait_ge(unit_taken, u.room(name))
                    return work[u.bank(name)]

                def product(bank, lhs, rhs):
                    passes = [(kt, i, j) for kt in range(KD) for i, j in ((0, 0), (0, 1), (1, 0))]
                    for n, (kt, i, j) in enumerate(passes):
                        last = nc.tensor.matmul(bank, lhs(i, kt), rhs(j, kt), start=(n == 0), stop=(n == len(passes) - 1))
                    last.then_inc(unit_ready, 1)

                def turn_x(b, u):
                    for kt in range(KD):
                        bank = room(u, f"T{kt}")
                        for tt in range(TT):
                            if kt == 0:
                                pe.wait_ge(normed, b * TT + (tt + 1))
                            last = nc.tensor.transpose(bank[:, tt * P:tt * P + P], xa[:, tt, kt * P:kt * P + P], ident[:, :])
                        last.then_inc(unit_ready, 1)

                def project_k(b, u):
                    pe.wait_ge(h_split, b * KD + KD)
                    product(room(u, "K")[:, :], lambda i, kt: wk_t[i][:, kt, :], lambda j, kt: h[j][:, kt, :])

                def project_q(b, g, u):
                    product(room(u, f"Q{g}")[:, :], lambda i, kt: wq_t[i][:, kt, g * P:g * P + P], lambda j, kt: h[j][:, kt, :])

                def project_v(b, u):
                    product(room(u, "V")[:, :], lambda i, kt: wv_t[i][:, kt, :], lambda j, kt: h[j][:, kt, :])

                def turn_v(b, u):
                    bank = room(u, "VT")
                    pe.wait_ge(unit_taken, u.done("V"))
                    for tt in range(TT):
                        last = nc.tensor.transpose(bank[:, tt * P:tt * P + P], v_full[:, tt * P:tt * P + P], ident[:, :])
                    last.then_inc(unit_ready, 1)

                def row_scores(b, g, i, u):
                    if i == 0:
                        pe.wait_ge(q_stacked[g % 2], stacked(b, g))
                        if g == 0:
                            pe.wait_ge(k_stacked, b * STACKED + STACKED)
                    r, qt = i // TT, i % TT
                    nc.tensor.matmul(room(u, f"S{g}_{i}")[:, :], q_stack[0:STACK, g, r, qt * P:qt * P + P],
                                     k_stack[0:STACK, g, :], start=True, stop=True).then_inc(unit_ready, 1)

                def turn_max(b, g, u):
                    bank = room(u, f"M{g}")
                    pe.wait_ge(unit_taken, u.before(f"M{g}"))
                    nc.tensor.transpose(bank[0:R * TT, 0:P], neg_max[:, g % 2, :], ident[:, :]).then_inc(unit_ready, 1)

                def scores(b, g, kt, is_first):
                    t = tile_no(b, g, kt)
                    if kt == 0:
                        pe.wait_ge(max_stacked, group_no(b, g) * 32 + 32)
                    for p in range(2):
                        if not (is_first and g == 0 and kt == 0):
                            pe.wait_ge(exp_done, t * 2 + (p - 1))
                        for i in range(2):
                            last = nc.tensor.matmul(pair[p][:, i, :], k_stack[0:SHIFT, g, kt * P:kt * P + P],
                                                    q_stack[0:SHIFT, g, 2 * p + i, :], start=True, stop=True)
                        last.then_inc(pair_ready, 1)

                def values(b, g, kt, is_first):
                    pe.wait_ge(exp_done, tile_no(b, g, kt) * 2 + 2)
                    if kt == 0 and not (is_first and g == 0):
                        pe.wait_ge(pv_copied, group_no(b, g))
                    for r in range(R):
                        last = nc.tensor.matmul(pv_bank[HD * r:HD * r + HD, :], v[:, kt, g * HD:g * HD + HD],
                                                probs[kt][:, r, :], start=(kt == 0), stop=(kt == TT - 1))
                    last.then_inc(pv_done, 1)

                def sums(b, g, is_first):
                    pe.wait_ge(added, group_no(b, g) * (TT - 1) + (TT - 1))
                    if not (is_first and g == 0):
                        pe.wait_ge(sums_taken, group_no(b, g))
                    for r in range(R):
                        last = nc.tensor.matmul(sum_bank[HD * r:HD * r + HD, :], ones[:, :], probs_sum[:, r, :],
                                                start=True, stop=True)
                    last.then_inc(sums_ready, 1)

                def project_out(b, tt, u):
                    bank = room(u, f"O{tt}")
                    if tt == 0:
                        pe.wait_ge(attn_split, b * HKV + HKV)
                    product(bank[:, :], lambda i, g: attn[i][:, g, tt * P:tt * P + P], lambda j, g: wo_t[j][:, g, :])

                def first():
                    u = first_units()
                    turn_x(0, u)
                    project_k(0, u)
                    for g in range(HKV):
                        project_q(0, g, u)
                    project_v(0, u)
                    turn_v(0, u)
                    pe.wait_ge(consts_ready, 2)
                    for i in range(R * TT):
                        row_scores(0, 0, i, u)
                    turn_max(0, 0, u)

                def sequence(b, is_first, has_next=True):
                    u = seq_units(b, has_next)
                    for g in range(HKV):
                        if g == 0:
                            pe.wait_ge(unit_taken, u.base)
                        for kt in range(TT):
                            scores(b, g, kt, is_first)
                            if kt == 2 and g > 0:
                                sums(b, g - 1, is_first)
                            if g + 1 < HKV:
                                for i in range(4 * kt, 4 * kt + 4):
                                    row_scores(b, g + 1, i, u)
                            if kt > 0:
                                values(b, g, kt - 1, is_first)
                            if kt == TT - 1 and g + 1 < HKV:
                                turn_max(b, g + 1, u)
                            if has_next:
                                for name in FILL.get((g, kt), []):
                                    if name == "T0":
                                        turn_x(b + 1, u)
                                    elif name == "K":
                                        project_k(b + 1, u)
                                    elif name[0] == "Q":
                                        project_q(b + 1, int(name[1]), u)
                        values(b, g, TT - 1, is_first)
                    if has_next:
                        project_q(b + 1, 3, u)
                        for i in range(4):
                            row_scores(b + 1, 0, i, u)
                        project_v(b + 1, u)
                        turn_v(b + 1, u)
                    sums(b, HKV - 1, is_first)
                    if has_next:
                        for i in range(4, 12):
                            row_scores(b + 1, 0, i, u)
                    project_out(b, 0, u)
                    if has_next:
                        for i in range(12, 16):
                            row_scores(b + 1, 0, i, u)
                    project_out(b, 1, u)
                    if has_next:
                        turn_max(b + 1, 0, u)
                    project_out(b, 2, u)
                    project_out(b, 3, u)

                sequences(pe, first, sequence, lambda b: sequence(b, False, has_next=False))


def mlp(nc, f32, f32r, ALU, ACT, sb, ps, sem, as_f32, seq_dram, ident, cond_cols, bias_cols, neg_half,
        w1, w2, b2, x1_dram, gate_dram, out):
    RING = 3
    with ExitStack() as st:
        w1_t = [sb(st, f"w1_t{i}", [P, KD, DFF], f32r) for i in range(2)]
        w2_t = [sb(st, f"w2_t{i}", [P, NJ, D], f32r) for i in range(2)]
        w1_in = [sb(st, f"w1_in{i}", [P, D]) for i in range(RING)]
        w2_in = [sb(st, f"w2_in{i}", [P, KD, P]) for i in range(RING)]
        xb = sb(st, "xb", [P, TT, D])
        stats = sb(st, "stats2", [P, TT, 6])
        mean_var = sb(st, "mean_var2", [P, TT, 2])
        var_eps = sb(st, "var_eps2", [P, TT])
        rstd = sb(st, "rstd2", [P, TT])
        shift_col = sb(st, "shift_col2", [P, TT])
        cond_now = sb(st, "cond_now2", [P, NC])
        h_full = [sb(st, f"h2_full{i}", [P, N]) for i in range(2)]
        h = [sb(st, f"h2_{i}", [P, KD, N], f32r) for i in range(2)]
        gelu_full = [sb(st, f"gelu_full{i}", [P, N]) for i in range(2)]
        hidden = [[sb(st, f"hidden{s}{i}", [P, N], f32r) for i in range(2)] for s in range(2)]
        resid = sb(st, "resid2", [P, TT, D])
        y = sb(st, "y", [P, TT, D])
        gate_now = sb(st, "gate_now2", [P, D])
        b2_rows = sb(st, "b2_rows", [P, D])

        acc = [ps(st, f"acc{i}", [P, D]) for i in range(TT)]
        up = [ps(st, f"up{i}", [P, N]) for i in range(2)]
        turn = [ps(st, f"turn{i}", [P, N]) for i in range(2)]

        w_loaded = [sem(f"w_ring{i}") for i in range(RING)]
        x_loaded, stats_done, moments_done, eps_added = sem("x_loaded2"), sem("stats_done2"), sem("moments_done2"), sem("eps_added2")
        rstd_ready, shift_ready, normed, cond_copied = sem("rstd_ready2"), sem("shift_ready2"), sem("normed2"), sem("cond_copied2")
        turned, turn_free, h_ready, h_hi, h_split = sem("turned"), sem("turn_free"), sem("h_ready2"), sem("h_hi2"), sem("h_split2")
        w_turned, w_hi, w_split = sem("w_turned2"), sem("w_hi2"), sem("w_split2")
        up_ready, gelu_done, hid_hi, hid_split, down_done = sem("up_ready"), sem("gelu_done"), sem("hid_hi"), sem("hid_split"), sem("down_done")
        acc_ready, acc_taken, y_gated, y_added = sem("acc_ready"), sem("acc_taken"), sem("y_gated"), sem("y_added")
        b2_loaded, gate_loaded, resid_loaded, out_stored = sem("b2_loaded"), sem("gate_loaded2"), sem("resid_loaded2"), sem("out_stored")

        def sequences(eng, body):
            body(0, True, True)
            with eng.Fori(1, B - 1) as b:
                body(b, False, True)
            body(B - 1, False, False)

        with nc.Block() as block:
            @block.sync
            def _(sp):
                def body(b, is_first, has_next):
                    if is_first:
                        sp.dma_start(xb[:, :, :], seq_dram(x1_dram, b)).then_inc(x_loaded, 16)
                        sp.dma_start(b2_rows[:, :], b2.rearrange("(a d) -> a d", a=1).partition_broadcast(P).rearrange("p a d -> p (a d)")).then_inc(b2_loaded, 16)
                        for j in range(NJ):
                            if j == RING:
                                load_next(b)
                            if j >= RING:
                                sp.wait_ge(w_turned, 2 * (j - RING) + 2)
                            sp.dma_start(w1_in[j % RING][:, :], w1[j * P:j * P + P, :]).then_inc(w_loaded[j % RING], 16)
                            sp.dma_start(w2_in[j % RING][:, :, :],
                                         w2[:, j * P:j * P + P].rearrange("(o p) i -> p o i", p=P)).then_inc(w_loaded[j % RING], 16)
                    elif has_next:
                        load_next(b)
                    if not is_first:
                        store(b - 1)
                    sp.dma_start(gate_now[:, :], gate_dram[bass.ds(b, 1), 1, :].partition_broadcast(P).rearrange("p a d -> p (a d)")).then_inc(gate_loaded, 16)
                    sp.dma_start(resid[:, :, :], seq_dram(x1_dram, b)).then_inc(resid_loaded, 16)
                    if not has_next:
                        store(b)

                def load_next(b):
                    sp.wait_ge(turned, b * KD + KD)
                    sp.dma_start(xb[:, :, :], seq_dram(x1_dram, b + 1)).then_inc(x_loaded, 16)

                def store(b):
                    sp.wait_ge(y_added, b * TT + TT)
                    sp.dma_start(seq_dram(out, b), y[:, :, :]).then_inc(out_stored, 16)
                    sp.wait_ge(out_stored, b * 16 + 16)

                sequences(sp, body)

            @block.gpsimd
            def _(pool):
                def rstd_of(b):
                    pool.wait_ge(eps_added, b + 1)
                    nc.gpsimd.tensor_tensor(rstd[:, :], var_eps[:, :], neg_half[:, :], ALU.pow).then_inc(rstd_ready, 1)

                def body(b, is_first, has_next):
                    if is_first:
                        rstd_of(0)
                    if has_next:
                        rstd_of(b + 1)
                    pool.wait_ge(gate_loaded, b * 16 + 16)
                    pool.wait_ge(resid_loaded, b * 16 + 16)
                    for tt in range(TT):
                        n = b * TT + (tt + 1)
                        pool.wait_ge(acc_taken, n)
                        nc.gpsimd.tensor_tensor(y[:, tt, :], y[:, tt, :], gate_now[:, :], ALU.mult).then_inc(y_gated, 1)
                        pool.wait_ge(y_gated, n)
                        nc.gpsimd.tensor_tensor(y[:, tt, :], y[:, tt, :], resid[:, tt, :], ALU.add).then_inc(y_added, 1)

                sequences(pool, body)

            @block.scalar
            def _(act):
                def norm(b):
                    act.wait_ge(shift_ready, b + 1)
                    for tt in range(TT):
                        nc.scalar.activation(xb[:, tt, :], xb[:, tt, :], ACT.Identity, scale=rstd[:, tt:tt + 1],
                                             bias=shift_col[:, tt:tt + 1]).then_inc(normed, 1)

                def modulate(b, kt, is_first=False):
                    if kt == 0:
                        act.wait_ge(cond_copied, b + 1)
                    act.wait_ge(turned, b * KD + (kt + 1))
                    if not (is_first and kt < 2):
                        act.wait_ge(h_split, b * KD + (kt - 1))
                    nc.scalar.activation(h_full[kt % 2][:, :], turn[kt % 2][:, :], ACT.Identity,
                                         scale=cond_now[:, SC2 + kt:SC2 + kt + 1],
                                         bias=cond_now[:, SH2 + kt:SH2 + kt + 1]).then_inc(h_ready, 1)

                def weights_high(j):
                    act.wait_ge(w_turned, 2 * j + 1)
                    nc.scalar.activation(w1_t[0][:, :, j * P:j * P + P], turn[0][:, :].rearrange("p (k n) -> p k n", k=KD),
                                         ACT.Copy).then_inc(w_hi, 1)
                    act.wait_ge(w_turned, 2 * j + 2)
                    nc.scalar.activation(w2_t[0][:, j, :], turn[1][:, :], ACT.Copy).then_inc(w_hi, 1)

                def body(b, is_first, has_next):
                    if is_first:
                        norm(0)
                        for kt in range(KD):
                            modulate(0, kt, is_first=True)
                        weights_high(0)
                    for j in range(NJ):
                        t = b * NJ + j
                        if is_first and j + 1 < NJ:
                            weights_high(j + 1)
                        act.wait_ge(up_ready, t + 1)
                        if not (is_first and j < 2):
                            act.wait_ge(hid_split, t - 1)
                        nc.scalar.activation(gelu_full[j % 2][:, :], up[j % 2][:, :], ACT.Gelu,
                                             bias=bias_cols[:, NC + j:NC + j + 1]).then_inc(gelu_done, 1)
                        if has_next and j == 9:
                            norm(b + 1)
                    if has_next:
                        for kt in range(KD):
                            modulate(b + 1, kt)

                sequences(act, body)

            @block.vector
            def _(dve):
                def tile_stats(b):
                    nc.vector.tensor_copy(cond_now[:, :], cond_cols[:, bass.ds(b, 1), :].rearrange("p a j -> p (a j)")).then_inc(cond_copied, 1)
                    dve.wait_ge(x_loaded, b * 16 + 16)
                    for tt in range(TT):
                        nc.vector.bn_stats(stats[:, tt, :], xb[:, tt, :]).then_inc(stats_done, 1)

                def moments(b):
                    for tt in range(TT):
                        nc.vector.bn_aggr(mean_var[:, tt, :], stats[:, tt, :]).then_inc(moments_done, 1)
                    dve.wait_ge(moments_done, b * TT + TT)
                    nc.vector.tensor_scalar(var_eps[:, :], mean_var[:, :, 1], EPS, None, ALU.add).then_inc(eps_added, 1)

                def shift_of(b):
                    dve.wait_ge(rstd_ready, b + 1)
                    nc.vector.scalar_tensor_tensor(out=shift_col[:, :], in0=mean_var[:, :, 0], scalar=-1.0,
                                                   in1=rstd[:, :], op0=ALU.mult, op1=ALU.mult).then_inc(shift_ready, 1)

                def split_h(b, kt):
                    n = b * KD + (kt + 1)
                    dve.wait_ge(h_ready, n)
                    nc.vector.tensor_copy(h[0][:, kt, :], h_full[kt % 2][:, :]).then_inc(h_hi, 1)
                    dve.wait_ge(h_hi, n)
                    nc.vector.tensor_tensor(h[1][:, kt, :], h_full[kt % 2][:, :], as_f32(h[0][:, kt, :]),
                                            ALU.subtract).then_inc(h_split, 1)

                def weights_low(j):
                    dve.wait_ge(w_hi, 2 * j + 1)
                    nc.vector.tensor_tensor(w1_t[1][:, :, j * P:j * P + P], turn[0][:, :].rearrange("p (k n) -> p k n", k=KD),
                                            as_f32(w1_t[0][:, :, j * P:j * P + P]), ALU.subtract).then_inc(w_split, 1)
                    dve.wait_ge(w_hi, 2 * j + 2)
                    nc.vector.tensor_tensor(w2_t[1][:, j, :], turn[1][:, :], as_f32(w2_t[0][:, j, :]),
                                            ALU.subtract).then_inc(w_split, 1)

                def split_hidden(b, j, is_first):
                    n = b * NJ + (j + 1)
                    dve.wait_ge(gelu_done, n)
                    if j >= 2:
                        dve.wait_ge(down_done, b * (NJ - 1) + (j - 1))
                    elif not is_first:
                        dve.wait_ge(*((down_done, b * (NJ - 1)) if j == 0 else (acc_ready, b * TT)))
                    nc.vector.tensor_copy(hidden[j % 2][0][:, :], gelu_full[j % 2][:, :]).then_inc(hid_hi, 1)
                    dve.wait_ge(hid_hi, n)
                    nc.vector.tensor_tensor(hidden[j % 2][1][:, :], gelu_full[j % 2][:, :], as_f32(hidden[j % 2][0][:, :]),
                                            ALU.subtract).then_inc(hid_split, 1)

                def take_acc(b, is_first):
                    if not is_first:
                        dve.wait_ge(out_stored, b * 16)
                    for tt in range(TT):
                        dve.wait_ge(acc_ready, b * TT + (tt + 1))
                        nc.vector.tensor_tensor(y[:, tt, :], acc[tt][:, :], b2_rows[:, :], ALU.add).then_inc(acc_taken, 1)

                def body(b, is_first, has_next):
                    if is_first:
                        tile_stats(0)
                        dve.wait_ge(stats_done, TT)
                        moments(0)
                        shift_of(0)
                        for kt in range(KD):
                            split_h(0, kt)
                        weights_low(0)
                        dve.wait_ge(b2_loaded, 16)
                    for j in range(NJ):
                        if is_first and j + 1 < NJ:
                            weights_low(j + 1)
                        if has_next and j == 6:
                            dve.wait_ge(stats_done, b * TT + 2 * TT)
                        split_hidden(b, j, is_first)
                        if has_next and j == 5:
                            tile_stats(b + 1)
                        if has_next and j == 6:
                            moments(b + 1)
                        if has_next and j == 8:
                            shift_of(b + 1)
                    if has_next:
                        dve.wait_ge(up_ready, b * NJ + NJ)
                        for kt in range(KD):
                            split_h(b + 1, kt)
                    take_acc(b, is_first)

                sequences(dve, body)

            @block.tensor
            def _(pe):
                PASSES = ((0, 0), (0, 1), (1, 0))

                def turn_x(b, kt, is_first=False):
                    if is_first:
                        if kt >= 2:
                            pe.wait_ge(h_ready, kt - 1)
                    elif kt >= 2:
                        pe.wait_ge(h_ready, b * KD + (kt - 1))
                    else:
                        pe.wait_ge(h_ready, b * KD)
                        pe.wait_ge(w_split, 2 * NJ)
                    for tt in range(TT):
                        if kt == 0:
                            pe.wait_ge(normed, b * TT + (tt + 1))
                        last = nc.tensor.transpose(turn[kt % 2][:, tt * P:tt * P + P], xb[:, tt, kt * P:kt * P + P], ident[:, :])
                    last.then_inc(turned, 1)

                def turn_weights(j):
                    pe.wait_ge(w_loaded[j % RING], 32 * (j // RING) + 32)
                    if j == 0:
                        pe.wait_ge(h_ready, KD)
                    else:
                        pe.wait_ge(w_split, 2 * j - 1)
                    for kt in range(KD):
                        last = nc.tensor.transpose(turn[0][:, kt * P:kt * P + P], w1_in[j % RING][:, kt * P:kt * P + P], ident[:, :])
                    last.then_inc(w_turned, 1)
                    if j > 0:
                        pe.wait_ge(w_split, 2 * j)
                    for o in range(KD):
                        last = nc.tensor.transpose(turn[1][:, o * P:o * P + P], w2_in[j % RING][:, o, :], ident[:, :])
                    last.then_inc(w_turned, 1)

                def up_product(b, j, is_first):
                    if j == 0:
                        pe.wait_ge(h_split, b * KD + KD)
                    if is_first:
                        pe.wait_ge(w_split, 2 * j + 2)
                    if not (is_first and j < 2):
                        pe.wait_ge(gelu_done, b * NJ + (j - 1))
                    for kt in range(KD):
                        for n, (i, k) in enumerate(PASSES):
                            last = nc.tensor.matmul(up[j % 2][:, :], w1_t[i][:, kt, j * P:j * P + P], h[k][:, kt, :],
                                                    start=(kt == 0 and n == 0), stop=(kt == KD - 1 and n == 2))
                    last.then_inc(up_ready, 1)

                def down_product(b, j, is_first):
                    pe.wait_ge(hid_split, b * NJ + (j + 1))
                    for tt in range(TT):
                        if j == 0 and not is_first:
                            pe.wait_ge(acc_taken, b * TT - TT + (tt + 1))
                        for n, (i, k) in enumerate(PASSES):
                            last = nc.tensor.matmul(acc[tt][:, :], hidden[j % 2][i][:, tt * P:tt * P + P], w2_t[k][:, j, :],
                                                    start=(j == 0 and n == 0), stop=(j == NJ - 1 and n == 2))
                        if j == NJ - 1:
                            last.then_inc(acc_ready, 1)
                    if j < NJ - 1:
                        last.then_inc(down_done, 1)

                def body(b, is_first, has_next):
                    if is_first:
                        for kt in range(KD):
                            turn_x(0, kt, is_first=True)
                        turn_weights(0)
                    for j in range(NJ):
                        if is_first and j + 1 < NJ:
                            turn_weights(j + 1)
                        up_product(b, j, is_first)
                        if j >= 1:
                            down_product(b, j - 1, is_first)
                        if has_next and j == NJ - 2:
                            turn_x(b + 1, 0)
                            turn_x(b + 1, 1)
                    down_product(b, NJ - 1, is_first)
                    if has_next:
                        turn_x(b + 1, 2)
                        turn_x(b + 1, 3)

                sequences(pe, body)


_INS = ["x", "cond_1024", "L0_cond_wq", "L0_cond_wk", "L0_cond_wv", "L0_cond_wo", "L0_cond_w1", "L0_cond_b1",
        "L0_cond_w2", "L0_cond_b2", "L0_cond_wc", "L0_cond_bc"]


def kernel(**inputs):
    import numpy as _np
    import concourse.bacc as _bacc
    from concourse import mybir as _mybir
    from concourse.bass_utils import run_bass_kernel_spmd as _run

    nc = _bacc.Bacc("TRN2", target_bir_lowering=False, num_devices=1)
    arrays, args = {}, []
    for name in _INS:
        a = _np.ascontiguousarray(inputs[name])
        arrays[f"in_{name}_dram"] = a
        args.append(nc.dram_tensor(f"in_{name}_dram", a.shape, _mybir.dt.from_np(a.dtype), kind="ExternalInput").ap())
    out = nc.dram_tensor("out_0_dram", (B, N, D), _mybir.dt.float32, kind="ExternalOutput").ap()
    layer_kernel(nc, *args, out)
    r = _run(nc, [arrays], core_ids=[0])
    return r.results[0]["out_0_dram"]
```

```python
import concourse.bass as bass
from concourse import mybir
from contextlib import ExitStack


P = 128
B, N, D = 8, 512, 512
HKV, R, HD = 4, 4, 32
DFF = 2048
TT = N // P
KD = D // P
NJ = DFF // P
NC = 6 * KD
SH1, SC1, G1, SH2, SC2, G2 = (i * KD for i in range(6))
EPS = 1e-5
SCORE_SCALE = 1.0 / float(HD) ** 0.5
STACK = 3 * HD
SHIFT = STACK + 2

FILL = {(0, 0): ["VT", "Q2"], (0, 3): ["Q3"], (1, 0): ["O0"], (1, 1): ["O1"], (1, 2): ["O2"], (1, 3): ["O3"],
        (2, 0): ["T0", "T1", "T2", "T3"], (2, 1): ["K"], (2, 2): ["Q0"], (2, 3): ["Q1"], (3, 3): ["V"]}
ROWS_IN_SLOT = [5, 5, 4, 2]
FIRST_ROW = [sum(ROWS_IN_SLOT[:i]) for i in range(TT)]
TAKER = {"T": "act", "V": "act", "K": "dve", "Q": "dve", "O": "dve"}


def fill(g, kt, has_last, has_next):
    return [n for n in FILL.get((g, kt), [])
            if (has_last or n[0] != "O") and (has_next or n not in ("T0", "T1", "T2", "T3", "K", "Q0", "Q1", "V"))]


class Units:

    def __init__(self, order, base):
        self.at = {name: i for i, name in enumerate(order)}
        self.order, self.base = order, base

    def bank(self, name):
        return self.at[name] % 2

    def ready(self, name):
        return self.base["all"] + (self.at[name] + 1)

    def taken(self, name):
        who = TAKER[name[0]]
        mine = [n for n in self.order if TAKER[n[0]] == who]
        return self.base[who] + (mine.index(name) + 1)

    def after(self):
        return {k: self.base[k] + n for k, n in sizes(self.order).items()}


def sizes(order):
    return {"all": len(order), "act": sum(TAKER[n[0]] == "act" for n in order),
            "dve": sum(TAKER[n[0]] == "dve" for n in order)}


def seq_order(has_last, has_next):
    return [n for g in range(HKV) for kt in range(TT) for n in fill(g, kt, has_last, has_next)]


def before_units():
    return Units(["T0", "T1", "T2", "T3", "K", "Q0", "Q1", "V"], {"all": 0, "act": 0, "dve": 0})


def seq_units(b, has_last, has_next):
    ahead = before_units().after()
    if has_last:
        ahead = Units(seq_order(False, True), ahead).after()
        step = sizes(seq_order(True, True))
        ahead = {k: (b - 1) * step[k] + ahead[k] for k in ahead}
    return Units(seq_order(has_last, has_next), ahead)


def after_units():
    return Units(["O0", "O1", "O2", "O3"], seq_units(B - 1, True, False).after())


ROWS = R * TT


def row_no(b, g, i):
    return b * (HKV * (ROWS + 1)) + (g * (ROWS + 1) + i)


def layer_kernel(nc, x, cond, wq, wk, wv, wo, w1, b1, w2, b2, wc, bc, out):
    f32, f32r = mybir.dt.float32, mybir.dt.float32r
    ALU, ACT, AX = mybir.AluOpType, mybir.ActivationFunctionType, mybir.AxisListType

    x1_dram = nc.dram_tensor("x1_scratch", (B, N, D), f32, kind="Internal").ap()
    gate_dram = nc.dram_tensor("gate_scratch", (B, 2, D), f32, kind="Internal").ap()

    def seq_dram(t, b):
        return t[bass.ds(b, 1), :, :].rearrange("a (t p) d -> p (a t) d", p=P)

    def as_f32(ap):
        return ap.bitcast(f32)

    with ExitStack() as ctx:
        def sb(stack, name, shape, dt=f32):
            return stack.enter_context(nc.sbuf_tensor(name, shape, dt))

        def ps(stack, name, shape, dt=f32):
            return stack.enter_context(nc.psum_tensor(name, shape, dt))

        def sem(name):
            return ctx.enter_context(nc.semaphore(name))

        ident = sb(ctx, "ident", [P, P])
        cond_cols = sb(ctx, "cond_cols", [P, B, NC])
        bias_cols = sb(ctx, "bias_cols", [P, NC + NJ])
        neg_half = sb(ctx, "neg_half", [P, TT])

        attn_ctx = ExitStack()
        with attn_ctx:
            wq_t = [sb(attn_ctx, f"wq_t{i}", [P, KD, D], f32r) for i in range(2)]
            wk_t = [sb(attn_ctx, f"wk_t{i}", [P, KD, P], f32r) for i in range(2)]
            wv_t = [sb(attn_ctx, f"wv_t{i}", [P, KD, P], f32r) for i in range(2)]
            wo_t = [sb(attn_ctx, f"wo_t{i}", [P, KD, D], f32r) for i in range(2)]

            prologue(nc, f32, f32r, ALU, ACT, sb, ps, sem, ident, cond_cols, bias_cols, neg_half,
                     wq_t, wk_t, wv_t, wo_t, cond, wq, wk, wv, wo, b1, wc, bc, gate_dram)
            attention(nc, f32, f32r, ALU, ACT, AX, sb, ps, sem, as_f32, seq_dram, ident, cond_cols, neg_half,
                      wq_t, wk_t, wv_t, wo_t, x, x1_dram, gate_dram)
        mlp(nc, f32, f32r, ALU, ACT, sb, ps, sem, as_f32, seq_dram, ident, cond_cols, bias_cols, neg_half,
            w1, w2, b2, x1_dram, gate_dram, out)


def prologue(nc, f32, f32r, ALU, ACT, sb, ps, sem, ident, cond_cols, bias_cols, neg_half,
             wq_t, wk_t, wv_t, wo_t, cond, wq, wk, wv, wo, b1, wc, bc, gate_dram):
    with ExitStack() as st:
        c_row = sb(st, "c_row", [B, D])
        silu_row = sb(st, "silu_row", [B, D])
        silu_t = sb(st, "silu_t", [P, KD, B])
        bias_rows = sb(st, "bias_rows", [NC + NJ, P])
        wc_in = sb(st, "wc_in", [P, NC, D])
        wc_turned = [sb(st, f"wc_turned{i}", [P, KD, P]) for i in range(4)]
        gate_rows = sb(st, "gate_rows", [B, 2, D])
        attn_in = {"q": sb(st, "wq_in", [P, KD, D]), "k": sb(st, "wk_in", [P, 1, D]),
                   "v": sb(st, "wv_in", [P, 1, D]), "o": sb(st, "wo_in", [P, KD, D])}
        wc_bank = [ps(st, f"wc_bank{i}", [P, D]) for i in range(4)]
        cond_bank = ps(st, "cond_bank", [P, NC, B])
        small_bank = ps(st, "small_bank", [P, D])
        w_bank = [ps(st, f"w_bank{i}", [P, D]) for i in range(2)]

        ident_zero, ident_ready = sem("ident_zero"), sem("ident_ready")
        c_loaded, bias_loaded = sem("c_loaded"), sem("bias_loaded")
        wc_loaded = [sem(f"wc_loaded{i}") for i in range(6)]
        w_loaded = {n: sem(f"w{n}_loaded") for n in "qkvo"}
        silu_done, silu_turned, silu_taken = sem("silu_done"), sem("silu_turned"), sem("silu_taken")
        bias_turned, bias_taken = sem("bias_turned"), sem("bias_taken")
        w_turned, w_hi, w_split = sem("w_turned"), sem("w_hi"), sem("w_split")
        wc_done = sem("wc_done")
        wc_taken = [sem("wc_taken_act"), sem("wc_taken_dve")]
        cond_done, cond_ready = sem("cond_done"), sem("cond_ready")
        gates_turned, gates_taken, gates_stored = sem("gates_turned"), sem("gates_taken"), sem("gates_stored")

        w_units = [("q", kt) for kt in range(KD)] + [("k", 0), ("v", 0)] + [("o", kt) for kt in range(KD)]
        w_dst = {"q": wq_t, "k": wk_t, "v": wv_t, "o": wo_t}

        def unit_dst(u, half):
            which, kt = w_units[u]
            return w_dst[which][half][:, kt, :] if which in "qo" else w_dst[which][half][:, :, :].rearrange("p k n -> p (k n)")

        with nc.Block() as block:
            @block.sync
            def _(sp):
                sp.dma_start(c_row[:, :], cond).then_inc(c_loaded, 16)
                sp.dma_start(bias_rows[0:NC, :], bc.rearrange("(j p) -> j p", p=P)).then_inc(bias_loaded, 16)
                sp.dma_start(bias_rows[NC:NC + NJ, :], b1.rearrange("(j p) -> j p", p=P)).then_inc(bias_loaded, 16)
                for n, w in (("q", wq), ("k", wk), ("v", wv), ("o", wo)):
                    sp.dma_start(attn_in[n][:, :, :], w.rearrange("(o p) i -> p o i", p=P)).then_inc(w_loaded[n], 16)
                for i in range(6):
                    sp.dma_start(wc_in[:, KD * i:KD * i + KD, :],
                                 wc[D * i:D * i + D, :].rearrange("(o p) i -> p o i", p=P)).then_inc(wc_loaded[i], 16)
                sp.wait_ge(gates_taken, 2)
                sp.dma_start(gate_dram, gate_rows[:, :, :]).then_inc(gates_stored, 16)
                sp.wait_ge(gates_stored, 16)

            @block.gpsimd
            def _(pool):
                nc.gpsimd.memset(ident[:, :], 0.0).then_inc(ident_zero, 1)
                pool.wait_ge(ident_zero, 1)
                nc.gpsimd.affine_select(out=ident[:, :], in_=ident[:, :], compare_op=ALU.not_equal, fill=1.0,
                                        base=0, pattern=[[-1, P]], channel_multiplier=1).then_inc(ident_ready, 1)
                nc.gpsimd.memset(neg_half[:, :], -0.5).then_inc(ident_zero, 1)

            @block.scalar
            def _(act):
                act.wait_ge(c_loaded, 16)
                nc.scalar.activation(silu_row[:, :], c_row[:, :], ACT.Silu).then_inc(silu_done, 1)
                for u in range(len(w_units)):
                    act.wait_ge(w_turned, u + 1)
                    nc.scalar.activation(unit_dst(u, 0), w_bank[u % 2][:, :], ACT.Copy).then_inc(w_hi, 1)
                for j in range(0, NC, 2):
                    act.wait_ge(wc_done, j + 1)
                    if j >= 4:
                        act.wait_ge(cond_done, j - 3)
                    nc.scalar.activation(wc_turned[j % 4][:, :, :].rearrange("p k n -> p (k n)"), wc_bank[j % 4][:, :],
                                         ACT.Copy).then_inc(wc_taken[0], 1)

            @block.vector
            def _(dve):
                dve.wait_ge(silu_turned, 1)
                nc.vector.tensor_copy(silu_t[:, :, :].rearrange("p k b -> p (k b)"),
                                      small_bank[:, 0:KD * B]).then_inc(silu_taken, 1)
                dve.wait_ge(bias_turned, 1)
                nc.vector.tensor_copy(bias_cols[:, :], small_bank[:, 0:NC + NJ]).then_inc(bias_taken, 1)
                for u in range(len(w_units)):
                    dve.wait_ge(w_hi, u + 1)
                    nc.vector.tensor_tensor(unit_dst(u, 1), w_bank[u % 2][:, :], unit_dst(u, 0).bitcast(f32),
                                            ALU.subtract).then_inc(w_split, 1)
                for j in range(1, NC, 2):
                    dve.wait_ge(wc_done, j + 1)
                    if j >= 4:
                        dve.wait_ge(cond_done, j - 3)
                    nc.vector.tensor_copy(wc_turned[j % 4][:, :, :].rearrange("p k n -> p (k n)"),
                                          wc_bank[j % 4][:, :]).then_inc(wc_taken[1], 1)
                dve.wait_ge(cond_done, NC)
                dve.wait_ge(bias_taken, 1)
                for j in range(NC):
                    one = 1.0 if j // KD in (1, 4) else 0.0
                    nc.vector.tensor_scalar(cond_cols[:, :, j], cond_bank[:, j, :], bias_cols[:, j:j + 1], one,
                                            ALU.add, ALU.add).then_inc(cond_ready, 1)
                for i in range(2):
                    dve.wait_ge(gates_turned, i + 1)
                    nc.vector.tensor_copy(gate_rows[:, i, :], w_bank[i][0:B, :]).then_inc(gates_taken, 1)

            @block.tensor
            def _(pe):
                pe.wait_ge(ident_ready, 1)
                pe.wait_ge(silu_done, 1)
                for kt in range(KD):
                    last = nc.tensor.transpose(small_bank[:, kt * B:kt * B + B], silu_row[:, kt * P:kt * P + P],
                                               ident[0:B, 0:B])
                last.then_inc(silu_turned, 1)
                pe.wait_ge(silu_taken, 1)
                pe.wait_ge(bias_loaded, 32)
                nc.tensor.transpose(small_bank[:, 0:NC + NJ], bias_rows[:, :],
                                    ident[0:NC + NJ, 0:NC + NJ]).then_inc(bias_turned, 1)
                for u, (which, kt) in enumerate(w_units):
                    pe.wait_ge(w_loaded[which], 16)
                    if u >= 2:
                        pe.wait_ge(w_split, u - 1)
                    for i in range(KD):
                        src = (attn_in[which][:, i, kt * P:kt * P + P] if which in "qo"
                               else attn_in[which][:, 0, i * P:i * P + P])
                        last = nc.tensor.transpose(w_bank[u % 2][:, i * P:i * P + P], src, ident[:, :])
                    last.then_inc(w_turned, 1)
                for j in range(NC + 1):
                    if j < NC:
                        pe.wait_ge(wc_loaded[j // KD], 16)
                        if j >= 4:
                            pe.wait_ge(wc_taken[j % 2], j // 2 - 1)
                        for kt in range(KD):
                            last = nc.tensor.transpose(wc_bank[j % 4][:, kt * P:kt * P + P],
                                                       wc_in[:, j, kt * P:kt * P + P], ident[:, :])
                        last.then_inc(wc_done, 1)
                    if j >= 1:
                        i = j - 1
                        pe.wait_ge(wc_taken[i % 2], i // 2 + 1)
                        for kt in range(KD):
                            last = nc.tensor.matmul(cond_bank[:, i, :], wc_turned[i % 4][:, kt, :], silu_t[:, kt, :],
                                                    start=(kt == 0), stop=(kt == KD - 1))
                        last.then_inc(cond_done, 1)
                pe.wait_ge(cond_ready, NC)
                pe.wait_ge(w_split, len(w_units))
                for i, j0 in enumerate((G1, G2)):
                    for kt in range(KD):
                        last = nc.tensor.transpose(w_bank[i][0:B, kt * P:kt * P + P], cond_cols[:, :, j0 + kt],
                                                   ident[:, :])
                    last.then_inc(gates_turned, 1)


def attention(nc, f32, f32r, ALU, ACT, AX, sb, ps, sem, as_f32, seq_dram, ident, cond_cols, neg_half,
              wq_t, wk_t, wv_t, wo_t, x, x1_dram, gate_dram):
    with ExitStack() as st:
        xa = sb(st, "xa", [P, TT, D])
        stats = sb(st, "stats", [P, TT, 6])
        mean_var = sb(st, "mean_var", [P, TT, 2])
        var_eps = sb(st, "var_eps", [P, TT])
        rstd = sb(st, "rstd", [P, TT])
        shift_col = sb(st, "shift_col", [P, TT])
        cond_now = sb(st, "cond_now", [P, NC])
        h_full = [sb(st, f"h_full{i}", [P, N]) for i in range(2)]
        h = [sb(st, f"h{i}", [P, KD, N], f32r) for i in range(2)]
        k_part = [sb(st, f"k_part{i}", [P, N], f32r) for i in range(2)]
        q_part = [[sb(st, f"q_part{s}{i}", [P, N], f32r) for i in range(2)] for s in range(2)]
        v_full = sb(st, "v_full", [P, N])
        v = sb(st, "v", [P, TT, P])
        k_stack = sb(st, "k_stack", [P, HKV, N], f32r)
        q_stack = sb(st, "q_stack", [P, HKV, R, N], f32r)
        neg_max = sb(st, "neg_max", [P, 2, ROWS])
        max_row = [sb(st, f"max_row{i}", [ROWS, P], f32r) for i in range(2)]
        probs = [sb(st, f"probs{i}", [P, R, N]) for i in range(TT)]
        probs_sum = sb(st, "probs_sum", [P, R, N])
        ones = sb(st, "ones", [P, HD])
        inverse = sb(st, "inverse", [P, N])
        refined = sb(st, "refined", [P, N])
        attn_raw = sb(st, "attn_raw", [P, N])
        attn_full = sb(st, "attn_full", [P, N])
        attn = [sb(st, f"attn{i}", [P, HKV, N], f32r) for i in range(2)]
        gated = [sb(st, f"gated{i}", [P, D]) for i in range(2)]
        resid = sb(st, "resid", [P, TT, D])
        gate_now = sb(st, "gate_now", [P, D])

        key_bank = [ps(st, f"key_bank{i}", [P, N]) for i in range(2)]
        row_bank = [ps(st, f"row_bank{i}", [P, N]) for i in range(2)]
        proj_bank = [ps(st, f"proj_bank{i}", [P, N]) for i in range(2)]
        pv_bank = ps(st, "pv_bank", [P, N])
        sum_bank = ps(st, "sum_bank", [P, N])

        proj_ready = sem("proj_ready")
        proj_taken = {"act": sem("proj_taken_act"), "dve": sem("proj_taken_dve")}
        row_ready, row_taken = sem("row_ready"), sem("row_taken")
        consts_ready = sem("consts_ready")
        x_loaded, stats_done, moments_done, eps_added = sem("x_loaded"), sem("stats_done"), sem("moments_done"), sem("eps_added")
        rstd_ready, shift_ready, normed, cond_copied = sem("rstd_ready"), sem("shift_ready"), sem("normed"), sem("cond_copied")
        h_hi, h_split, k_hi, q_hi = sem("h_hi"), sem("h_split"), sem("k_hi"), sem("q_hi")
        k_stacked = [sem(f"k_stacked{g}") for g in range(HKV)]
        q_stacked = [sem(f"q_stacked{i}") for i in range(2)]
        max_hi, max_stacked = sem("max_hi"), sem("max_stacked")
        keys_scored, exp_done, pv_done, pv_copied = sem("keys_scored"), sem("exp_done"), sem("pv_done"), sem("pv_copied")
        added, sums_ready, log_done, inverse_ready = sem("added"), sem("sums_ready"), sem("log_done"), sem("inverse_ready")
        sums_taken, refined_done, attn_scaled = sem("sums_taken"), sem("refined_done"), sem("attn_scaled")
        attn_hi, attn_split = sem("attn_hi"), sem("attn_split")
        gate_loaded, resid_loaded, x1_added, x1_stored = sem("gate_loaded"), sem("resid_loaded"), sem("x1_added"), sem("x1_stored")

        QUERIES, KEYS = 3 * R * 16, 3 * 16

        def group_no(b, g):
            return b * HKV + g

        def tile_no(b, g, kt):
            return b * (HKV * TT) + (g * TT + kt)

        def exps_no(b, g, kt):
            return b * (HKV * TT * R) + (g * TT + kt) * R

        def queries_stacked(b, g):
            return b * (HKV // 2 * QUERIES) + (g // 2 + 1) * QUERIES

        def rowed(b, g, has_next):
            if g + 1 < HKV:
                return b, g + 1
            return (b + 1, 0) if has_next else None

        def sequences(eng, before, sequence, after):
            before()
            sequence(0, False, True)
            with eng.Fori(1, B - 1) as b:
                sequence(b, True, True)
            sequence(B - 1, True, False)
            after(B - 1)

        with nc.Block() as block:
            @block.sync
            def _(sp):
                def load_x(b):
                    sp.dma_start(xa[:, :, :], seq_dram(x, b)).then_inc(x_loaded, 16)

                def load_resid(b):
                    sp.dma_start(gate_now[:, :], gate_dram[bass.ds(b, 1), 0, :].partition_broadcast(P)
                                 .rearrange("p a d -> p (a d)")).then_inc(gate_loaded, 16)
                    sp.dma_start(resid[:, :, :], seq_dram(x, b)).then_inc(resid_loaded, 16)

                def store_x1(b):
                    sp.wait_ge(x1_added, b * TT + TT)
                    sp.dma_start(seq_dram(x1_dram, b), resid[:, :, :]).then_inc(x1_stored, 16)
                    sp.wait_ge(x1_stored, b * 16 + 16)

                def stack_k(g):
                    for row, part in ((0, 0), (1, 0), (2, 1)):
                        sp.dma_start(as_f32(k_stack[HD * row:HD * row + HD, g, :]),
                                     as_f32(k_part[part][HD * g:HD * g + HD, :])).then_inc(k_stacked[g], 16)

                def stack_q(u, g):
                    sp.wait_ge(proj_taken["dve"], u.taken(f"Q{g}"))
                    for r in range(R):
                        for row, part in ((0, 0), (1, 1), (2, 0)):
                            sp.dma_start(as_f32(q_stack[HD * row:HD * row + HD, g, r, :]),
                                         as_f32(q_part[g % 2][part][HD * r:HD * r + HD, :])).then_inc(q_stacked[g % 2], 16)

                def stack_max(b, g):
                    sp.wait_ge(row_taken, row_no(b, g, ROWS) + 1)
                    for part in range(2):
                        row = as_f32(q_stack[STACK + part:STACK + part + 1, g, :, :])
                        sp.dma_start(row.rearrange("o r n -> o (r n)"), as_f32(max_row[part][:, :])).then_inc(max_stacked, 16)

                def before():
                    u = before_units()
                    load_x(0)
                    sp.wait_ge(proj_taken["dve"], u.taken("K"))
                    for g in range(HKV):
                        stack_k(g)
                    stack_q(u, 0)
                    stack_q(u, 1)
                    stack_max(0, 0)

                def sequence(b, has_last, has_next):
                    u = seq_units(b, has_last, has_next)
                    if has_last:
                        sp.wait_ge(keys_scored, exps_no(b, 0, 0))
                        stack_k(HKV - 1)
                    if has_next:
                        load_x(b + 1)
                    stack_q(u, 2)
                    stack_max(b, 1)
                    stack_q(u, 3)
                    stack_max(b, 2)
                    if has_last:
                        store_x1(b - 1)
                    load_resid(b)
                    if has_next:
                        sp.wait_ge(proj_taken["dve"], u.taken("K"))
                        stack_k(0)
                        stack_k(1)
                        stack_q(u, 0)
                    stack_max(b, 3)
                    if has_next:
                        stack_q(u, 1)
                        stack_k(2)
                        stack_max(b + 1, 0)

                sequences(sp, before, sequence, store_x1)

            @block.gpsimd
            def _(pool):
                def rstd_of(b):
                    pool.wait_ge(eps_added, b + 1)
                    nc.gpsimd.tensor_tensor(rstd[:, :], var_eps[:, :], neg_half[:, :], ALU.pow).then_inc(rstd_ready, 1)

                def add_probs(b, g, kt):
                    pool.wait_ge(exp_done, exps_no(b, g, kt) + R)
                    if kt > 1:
                        pool.wait_ge(added, group_no(b, g) * (TT - 1) + (kt - 1))
                    first_in = probs[0] if kt == 1 else probs_sum
                    nc.gpsimd.tensor_tensor(probs_sum[:, :, :], first_in[:, :, :], probs[kt][:, :, :],
                                            ALU.add).then_inc(added, 1)

                def add_resid(b, tt, u):
                    if tt == 0:
                        pool.wait_ge(resid_loaded, b * 16 + 16)
                    pool.wait_ge(proj_taken["dve"], u.taken(f"O{tt}"))
                    nc.gpsimd.tensor_tensor(resid[:, tt, :], resid[:, tt, :], gated[tt % 2][:, :],
                                            ALU.add).then_inc(x1_added, 1)

                def before():
                    nc.gpsimd.memset(as_f32(k_stack[STACK:SHIFT, :, :]), 1.0).then_inc(consts_ready, 1)
                    pool.wait_ge(consts_ready, 1)
                    nc.gpsimd.memset(ones[:, :], 1.0).then_inc(consts_ready, 1)
                    rstd_of(0)

                def sequence(b, has_last, has_next):
                    u = seq_units(b, has_last, has_next)
                    for g in range(HKV):
                        if has_last or g > 0:
                            pool.wait_ge(sums_ready, group_no(b, g))
                        for kt in range(TT):
                            if kt > 0:
                                add_probs(b, g, kt)
                            if g == 1 and has_last:
                                add_resid(b - 1, kt, u)
                        if g == 0 and has_next:
                            rstd_of(b + 1)

                def after(b):
                    for tt in range(TT):
                        add_resid(b, tt, after_units())

                sequences(pool, before, sequence, after)

            @block.scalar
            def _(act):
                def norm(b):
                    act.wait_ge(shift_ready, b + 1)
                    for tt in range(TT):
                        nc.scalar.activation(xa[:, tt, :], xa[:, tt, :], ACT.Identity, scale=rstd[:, tt:tt + 1],
                                             bias=shift_col[:, tt:tt + 1]).then_inc(normed, 1)

                def modulate(b, u, is_first=False):
                    act.wait_ge(cond_copied, b + 1)
                    for kt in range(KD):
                        act.wait_ge(proj_ready, u.ready(f"T{kt}"))
                        if not (is_first and kt < 2):
                            act.wait_ge(h_split, b * KD + (kt - 1))
                        nc.scalar.activation(h_full[kt % 2][:, :], proj_bank[u.bank(f"T{kt}")][:, :], ACT.Identity,
                                             scale=cond_now[:, SC1 + kt:SC1 + kt + 1],
                                             bias=cond_now[:, SH1 + kt:SH1 + kt + 1]).then_inc(proj_taken["act"], 1)
                        act.wait_ge(proj_taken["act"], u.taken(f"T{kt}"))
                        nc.scalar.activation(h[0][:, kt, :], h_full[kt % 2][:, :], ACT.Copy).then_inc(h_hi, 1)

                def k_high(b, u, is_first=False):
                    act.wait_ge(proj_ready, u.ready("K"))
                    if not is_first:
                        act.wait_ge(k_stacked[HKV - 1], b * KEYS)
                    nc.scalar.activation(k_part[0][:, :], proj_bank[u.bank("K")][:, :], ACT.Copy).then_inc(k_hi, 1)

                def q_high(b, g, u, is_first=False):
                    act.wait_ge(proj_ready, u.ready(f"Q{g}"))
                    if not (is_first and g < 2):
                        act.wait_ge(q_stacked[g % 2], queries_stacked(b, g) - QUERIES)
                    nc.scalar.activation(q_part[g % 2][0][:, :], proj_bank[u.bank(f"Q{g}")][:, :], ACT.Copy,
                                         scale=SCORE_SCALE).then_inc(q_hi, 1)

                def take_v(u):
                    act.wait_ge(proj_ready, u.ready("V"))
                    nc.scalar.activation(v_full[:, :], proj_bank[u.bank("V")][:, :], ACT.Copy).then_inc(proj_taken["act"], 1)

                def take_vt(b, u, has_last):
                    act.wait_ge(proj_ready, u.ready("VT"))
                    if has_last:
                        act.wait_ge(pv_done, tile_no(b, 0, 0))
                    nc.scalar.activation(v[:, :, :].rearrange("p t n -> p (t n)"), proj_bank[u.bank("VT")][:, :],
                                         ACT.Copy).then_inc(proj_taken["act"], 1)

                def max_high(b, g, is_first=False):
                    n = row_no(b, g, ROWS)
                    act.wait_ge(row_ready, n + 1)
                    if not is_first:
                        act.wait_ge(max_stacked, group_no(b, g) * 32)
                    nc.scalar.activation(max_row[0][:, :], row_bank[g % 2][0:ROWS, 0:P], ACT.Copy).then_inc(max_hi, 1)

                def exp(b, g, kt, r, has_last):
                    if r == 0 and (has_last or g > 0):
                        act.wait_ge(pv_done, tile_no(b, g, kt) - (TT - 1))
                        act.wait_ge(added, group_no(b, g) * (TT - 1) - (TT - 1) + max(kt, 1))
                    act.wait_ge(keys_scored, exps_no(b, g, kt) + (r + 1))
                    nc.scalar.activation(probs[kt][:, r, :], key_bank[r % 2][:, :], ACT.Exp).then_inc(exp_done, 1)

                def copy_pv(b, g, is_first=False):
                    act.wait_ge(pv_done, tile_no(b, g, TT - 1) + 1)
                    if not is_first:
                        act.wait_ge(attn_scaled, group_no(b, g))
                    nc.scalar.activation(attn_raw[:, :], pv_bank[:, :], ACT.Copy).then_inc(pv_copied, 1)

                def invert(b, g, is_first=False):
                    n = group_no(b, g)
                    act.wait_ge(sums_ready, n + 1)
                    if not is_first:
                        act.wait_ge(refined_done, n)
                    nc.scalar.activation(inverse[:, :], sum_bank[:, :], ACT.Ln).then_inc(log_done, 1)
                    act.wait_ge(log_done, n + 1)
                    nc.scalar.activation(inverse[:, :], inverse[:, :], ACT.Exp, scale=-1.0).then_inc(inverse_ready, 1)

                def attn_high(b, g):
                    act.wait_ge(attn_scaled, group_no(b, g) + 1)
                    nc.scalar.activation(attn[0][:, g, :], attn_full[:, :], ACT.Copy).then_inc(attn_hi, 1)

                def before():
                    u = before_units()
                    nc.scalar.preload_act_table_set("natural_log_exp_and_others")
                    norm(0)
                    modulate(0, u, is_first=True)
                    k_high(0, u, is_first=True)
                    q_high(0, 0, u, is_first=True)
                    q_high(0, 1, u, is_first=True)
                    take_v(u)
                    max_high(0, 0, is_first=True)

                def slot(b, g, kt, u, has_last, has_next):
                    prev = (b, g - 1) if g > 0 else (b - 1, HKV - 1) if has_last else None
                    first_group = (g == 1 and not has_last)
                    exp(b, g, kt, 0, has_last)
                    exp(b, g, kt, 1, has_last)
                    if prev and kt == 0:
                        copy_pv(*prev, is_first=first_group)
                    if prev and kt == 2:
                        invert(*prev, is_first=first_group)
                    if prev and kt == 3 and g != 1:
                        attn_high(*prev)
                    if (g, kt) == (2, 0):
                        if has_last:
                            act.wait_ge(proj_ready, u.ready("O3"))
                        attn_high(b, 0)
                    exp(b, g, kt, 2, has_last)
                    if kt == TT - 1 and rowed(b, g, has_next):
                        max_high(*rowed(b, g, has_next))
                    exp(b, g, kt, 3, has_last)
                    if has_next and (g, kt) == (1, 1):
                        norm(b + 1)
                    for name in fill(g, kt, has_last, has_next):
                        if name == "VT":
                            take_vt(b, u, has_last)
                        elif name == "V":
                            take_v(u)
                        elif name == "T0":
                            modulate(b + 1, u)
                        elif name == "K":
                            k_high(b + 1, u)
                        elif name[0] == "Q":
                            q_high(b if name in ("Q2", "Q3") else b + 1, int(name[1]), u)

                def sequence(b, has_last, has_next):
                    u = seq_units(b, has_last, has_next)
                    for g in range(HKV):
                        for kt in range(TT):
                            slot(b, g, kt, u, has_last, has_next)

                def after(b):
                    copy_pv(b, HKV - 1)
                    invert(b, HKV - 1)
                    attn_high(b, HKV - 1)

                sequences(act, before, sequence, after)

            @block.vector
            def _(dve):
                def copy_cond(b):
                    nc.vector.tensor_copy(cond_now[:, :], cond_cols[:, bass.ds(b, 1), :]
                                          .rearrange("p a j -> p (a j)")).then_inc(cond_copied, 1)

                def tile_stats(tiles):
                    for tt in tiles:
                        nc.vector.bn_stats(stats[:, tt, :], xa[:, tt, :]).then_inc(stats_done, 1)

                def moments(b):
                    for tt in range(TT):
                        nc.vector.bn_aggr(mean_var[:, tt, :], stats[:, tt, :]).then_inc(moments_done, 1)
                    dve.wait_ge(moments_done, b * TT + TT)
                    nc.vector.tensor_scalar(var_eps[:, :], mean_var[:, :, 1], EPS, None, ALU.add).then_inc(eps_added, 1)

                def shift_of(b):
                    dve.wait_ge(rstd_ready, b + 1)
                    nc.vector.scalar_tensor_tensor(out=shift_col[:, :], in0=mean_var[:, :, 0], scalar=-1.0,
                                                   in1=rstd[:, :], op0=ALU.mult, op1=ALU.mult).then_inc(shift_ready, 1)

                def h_low(b):
                    for kt in range(KD):
                        dve.wait_ge(h_hi, b * KD + (kt + 1))
                        nc.vector.tensor_tensor(h[1][:, kt, :], h_full[kt % 2][:, :], as_f32(h[0][:, kt, :]),
                                                ALU.subtract).then_inc(h_split, 1)

                def k_low(b, u):
                    dve.wait_ge(k_hi, b + 1)
                    nc.vector.tensor_tensor(k_part[1][:, :], proj_bank[u.bank("K")][:, :], as_f32(k_part[0][:, :]),
                                            ALU.subtract).then_inc(proj_taken["dve"], 1)

                def q_low(b, g, u):
                    dve.wait_ge(q_hi, group_no(b, g) + 1)
                    nc.vector.scalar_tensor_tensor(out=q_part[g % 2][1][:, :], in0=proj_bank[u.bank(f"Q{g}")][:, :],
                                                   scalar=SCORE_SCALE, in1=as_f32(q_part[g % 2][0][:, :]),
                                                   op0=ALU.mult, op1=ALU.subtract).then_inc(proj_taken["dve"], 1)

                def row_max(b, g, i):
                    dve.wait_ge(row_ready, row_no(b, g, i) + 1)
                    nc.vector.tensor_reduce(out=neg_max[:, g % 2, i:i + 1], in_=row_bank[(g + i) % 2][:, :], op=ALU.max,
                                            axis=AX.X, negate=True).then_inc(row_taken, 1)

                def max_low(b, g):
                    dve.wait_ge(max_hi, group_no(b, g) + 1)
                    nc.vector.tensor_tensor(max_row[1][:, :], row_bank[g % 2][0:ROWS, 0:P],
                                            as_f32(max_row[0][:, :]), ALU.subtract).then_inc(row_taken, 1)

                def divide(b, g, is_first=False):
                    n = group_no(b, g) + 1
                    dve.wait_ge(inverse_ready, n)
                    nc.vector.tensor_tensor(refined[:, :], sum_bank[:, :], inverse[:, :], ALU.mult).then_inc(sums_taken, 1)
                    dve.wait_ge(sums_taken, n)
                    nc.vector.scalar_tensor_tensor(out=refined[:, :], in0=refined[:, :], scalar=2.0, in1=inverse[:, :],
                                                   op0=ALU.subtract, op1=ALU.mult).then_inc(refined_done, 1)
                    dve.wait_ge(refined_done, n)
                    dve.wait_ge(pv_copied, n)
                    nc.vector.scalar_tensor_tensor(out=attn_full[:, :], in0=attn_raw[:, :], scalar=-1.0, in1=refined[:, :],
                                                   op0=ALU.mult, op1=ALU.mult).then_inc(attn_scaled, 1)

                def attn_low(b, g):
                    dve.wait_ge(attn_hi, group_no(b, g) + 1)
                    nc.vector.tensor_tensor(attn[1][:, g, :], attn_full[:, :], as_f32(attn[0][:, g, :]),
                                            ALU.subtract).then_inc(attn_split, 1)

                def gate(b, tt, u):
                    dve.wait_ge(proj_ready, u.ready(f"O{tt}"))
                    if tt == 0:
                        dve.wait_ge(gate_loaded, b * 16 + 16)
                    if tt >= 2:
                        dve.wait_ge(x1_added, b * TT + (tt - 1))
                    nc.vector.tensor_tensor(gated[tt % 2][:, :], proj_bank[u.bank(f"O{tt}")][:, :], gate_now[:, :],
                                            ALU.mult).then_inc(proj_taken["dve"], 1)

                def before():
                    u = before_units()
                    copy_cond(0)
                    dve.wait_ge(x_loaded, 16)
                    tile_stats(range(TT))
                    dve.wait_ge(stats_done, TT)
                    moments(0)
                    shift_of(0)
                    h_low(0)
                    k_low(0, u)
                    q_low(0, 0, u)
                    q_low(0, 1, u)
                    for i in range(ROWS):
                        row_max(0, 0, i)
                    max_low(0, 0)

                def slot(b, g, kt, u, has_last, has_next):
                    prev = (b, g - 1) if g > 0 else (b - 1, HKV - 1) if has_last else None
                    if has_next and (g, kt) == (0, 3):
                        dve.wait_ge(stats_done, b * TT + 2 * TT)
                    if rowed(b, g, has_next):
                        for i in range(FIRST_ROW[kt], FIRST_ROW[kt] + ROWS_IN_SLOT[kt]):
                            row_max(*rowed(b, g, has_next), i)
                        if kt == TT - 1:
                            max_low(*rowed(b, g, has_next))
                    if has_next:
                        if (g, kt) == (0, 1):
                            copy_cond(b + 1)
                            dve.wait_ge(x_loaded, b * 16 + 32)
                            tile_stats((0, 1))
                        if (g, kt) == (0, 2):
                            tile_stats((2, 3))
                        if (g, kt) == (0, 3):
                            moments(b + 1)
                        if (g, kt) == (1, 1):
                            shift_of(b + 1)
                    if prev and kt == 2:
                        divide(*prev)
                    if prev and kt == 3 and g != 1:
                        attn_low(*prev)
                    if (g, kt) == (2, 0):
                        attn_low(b, 0)
                    for name in fill(g, kt, has_last, has_next):
                        if name == "T0":
                            h_low(b + 1)
                        elif name == "K":
                            k_low(b + 1, u)
                        elif name[0] == "Q":
                            q_low(b if name in ("Q2", "Q3") else b + 1, int(name[1]), u)
                        elif name[0] == "O":
                            gate(b - 1, int(name[1]), u)

                def sequence(b, has_last, has_next):
                    u = seq_units(b, has_last, has_next)
                    for g in range(HKV):
                        for kt in range(TT):
                            slot(b, g, kt, u, has_last, has_next)

                def after(b):
                    divide(b, HKV - 1)
                    attn_low(b, HKV - 1)
                    for tt in range(TT):
                        gate(b, tt, after_units())

                sequences(dve, before, sequence, after)

            @block.tensor
            def _(pe):
                def room(u, name):
                    i = u.at[name]
                    if i >= 2:
                        back = u.order[i - 2]
                        pe.wait_ge(proj_taken[TAKER[back[0]]], u.taken(back))
                    elif not (isinstance(u.base["all"], int) and u.base["all"] == 0):
                        for who in ("act", "dve"):
                            pe.wait_ge(proj_taken[who], u.base[who])
                    return proj_bank[u.bank(name)]

                def product(bank, lhs, rhs, half):
                    for kt in range(KD // 2 * half, KD // 2 * (half + 1)):
                        for i, j in ((0, 0), (0, 1), (1, 0)):
                            last = nc.tensor.matmul(bank, lhs(i, kt), rhs(j, kt), start=(kt == 0 and (i, j) == (0, 0)),
                                                    stop=(kt == KD - 1 and (i, j) == (1, 0)))
                    if half == 1:
                        last.then_inc(proj_ready, 1)

                def turn_x(b, kt, u):
                    bank = room(u, f"T{kt}")
                    for tt in range(TT):
                        if kt == 0:
                            pe.wait_ge(normed, b * TT + (tt + 1))
                        last = nc.tensor.transpose(bank[:, tt * P:tt * P + P], xa[:, tt, kt * P:kt * P + P], ident[:, :])
                    last.then_inc(proj_ready, 1)

                def turn_v(u, v_taken):
                    bank = room(u, "VT")
                    pe.wait_ge(proj_taken["act"], v_taken)
                    for tt in range(TT):
                        last = nc.tensor.transpose(bank[:, tt * P:tt * P + P], v_full[:, tt * P:tt * P + P], ident[:, :])
                    last.then_inc(proj_ready, 1)

                def project_k(b, u, half):
                    if half == 0:
                        room(u, "K")
                        pe.wait_ge(h_split, b * KD + KD)
                    product(proj_bank[u.bank("K")][:, :], lambda i, kt: wk_t[i][:, kt, :], lambda j, kt: h[j][:, kt, :], half)

                def project_q(g, u, half):
                    if half == 0:
                        room(u, f"Q{g}")
                    product(proj_bank[u.bank(f"Q{g}")][:, :], lambda i, kt: wq_t[i][:, kt, g * P:g * P + P],
                            lambda j, kt: h[j][:, kt, :], half)

                def project_v(u, half):
                    if half == 0:
                        room(u, "V")
                    product(proj_bank[u.bank("V")][:, :], lambda i, kt: wv_t[i][:, kt, :], lambda j, kt: h[j][:, kt, :], half)

                def project_out(b, tt, u, half):
                    if half == 0:
                        room(u, f"O{tt}")
                        if tt == 0:
                            pe.wait_ge(attn_split, b * HKV + HKV)
                    product(proj_bank[u.bank(f"O{tt}")][:, :], lambda i, g: attn[i][:, g, tt * P:tt * P + P],
                            lambda j, g: wo_t[j][:, g, :], half)

                def rows(b, g, i):
                    if i == 0:
                        pe.wait_ge(q_stacked[g % 2], queries_stacked(b, g))
                        pe.wait_ge(k_stacked[g], b * KEYS + KEYS)
                    if not (isinstance(b, int) and b == 0 and g == 0 and i < 2):
                        pe.wait_ge(row_taken, row_no(b, g, i) - 1)
                    r, qt = i // TT, i % TT
                    nc.tensor.matmul(row_bank[(g + i) % 2][:, :], q_stack[0:STACK, g, r, qt * P:qt * P + P],
                                     k_stack[0:STACK, g, :], start=True, stop=True).then_inc(row_ready, 1)

                def turn_max(b, g):
                    pe.wait_ge(row_taken, row_no(b, g, ROWS))
                    nc.tensor.transpose(row_bank[g % 2][0:ROWS, 0:P], neg_max[:, g % 2, :], ident[:, :]).then_inc(row_ready, 1)

                def scores(b, g, kt, r, has_last):
                    if kt == 0 and r == 0:
                        pe.wait_ge(max_stacked, group_no(b, g) * 32 + 32)
                    if has_last or g > 0 or kt > 0 or r >= 2:
                        pe.wait_ge(exp_done, exps_no(b, g, kt) + (r - 1))
                    nc.tensor.matmul(key_bank[r % 2][:, :], k_stack[0:SHIFT, g, kt * P:kt * P + P],
                                     q_stack[0:SHIFT, g, r, :], start=True, stop=True).then_inc(keys_scored, 1)

                def values(b, g, kt, is_first=False):
                    pe.wait_ge(exp_done, exps_no(b, g, kt) + R)
                    if kt == 0 and not is_first:
                        pe.wait_ge(pv_copied, group_no(b, g))
                    for r in range(R):
                        last = nc.tensor.matmul(pv_bank[HD * r:HD * r + HD, :], v[:, kt, g * HD:g * HD + HD],
                                                probs[kt][:, r, :], start=(kt == 0), stop=(kt == TT - 1))
                    last.then_inc(pv_done, 1)

                def sums(b, g, is_first=False):
                    pe.wait_ge(added, group_no(b, g) * (TT - 1) + (TT - 1))
                    if not is_first:
                        pe.wait_ge(sums_taken, group_no(b, g))
                    for r in range(R):
                        last = nc.tensor.matmul(sum_bank[HD * r:HD * r + HD, :], ones[:, :], probs_sum[:, r, :],
                                                start=True, stop=True)
                    last.then_inc(sums_ready, 1)

                def before():
                    u = before_units()
                    for kt in range(KD):
                        turn_x(0, kt, u)
                    for half in range(2):
                        project_k(0, u, half)
                    for g in range(2):
                        for half in range(2):
                            project_q(g, u, half)
                    for half in range(2):
                        project_v(u, half)
                    pe.wait_ge(consts_ready, 2)
                    for i in range(ROWS):
                        rows(0, 0, i)
                    turn_max(0, 0)

                def do(name, half, b, u):
                    if name == "VT":
                        turn_v(u, u.base["act"])
                    elif name[0] == "T":
                        turn_x(b + 1, int(name[1]), u)
                    elif name == "K":
                        project_k(b + 1, u, half)
                    elif name == "V":
                        project_v(u, half)
                    elif name[0] == "Q":
                        project_q(int(name[1]), u, half)
                    else:
                        project_out(b - 1, int(name[1]), u, half)

                def slot(b, g, kt, u, has_last, has_next):
                    prev = (b, g - 1) if g > 0 else (b - 1, HKV - 1) if has_last else None
                    parts = [(name, half) for name in fill(g, kt, has_last, has_next)
                             for half in ((0,) if name[0] == "T" or name == "VT" else (0, 1))]
                    cut = (len(parts) + 1) // 2
                    to_row = list(range(FIRST_ROW[kt], FIRST_ROW[kt] + ROWS_IN_SLOT[kt])) if rowed(b, g, has_next) else []

                    def some_rows(n):
                        for _ in range(min(n, len(to_row))):
                            rows(*rowed(b, g, has_next), to_row.pop(0))

                    scores(b, g, kt, 0, has_last)
                    scores(b, g, kt, 1, has_last)
                    some_rows(2 if kt == TT - 1 else 1)
                    if kt > 0:
                        if (g, kt) == (0, 1):
                            pe.wait_ge(proj_taken["act"], u.taken("VT"))
                        values(b, g, kt - 1, is_first=not has_last and g == 0)
                    elif prev:
                        values(*prev, TT - 1)
                    some_rows(1)
                    scores(b, g, kt, 2, has_last)
                    scores(b, g, kt, 3, has_last)
                    some_rows(1)
                    if kt == TT - 1 and rowed(b, g, has_next):
                        turn_max(*rowed(b, g, has_next))
                    for name, half in parts[:cut]:
                        do(name, half, b, u)
                    some_rows(1)
                    for name, half in parts[cut:]:
                        do(name, half, b, u)
                    if kt == 1 and prev:
                        sums(*prev, is_first=not has_last and g == 1)
                    some_rows(1)

                def sequence(b, has_last, has_next):
                    u = seq_units(b, has_last, has_next)
                    for g in range(HKV):
                        for kt in range(TT):
                            slot(b, g, kt, u, has_last, has_next)

                def after(b):
                    values(b, HKV - 1, TT - 1)
                    sums(b, HKV - 1)
                    for tt in range(TT):
                        for half in range(2):
                            project_out(b, tt, after_units(), half)

                sequences(pe, before, sequence, after)


def mlp(nc, f32, f32r, ALU, ACT, sb, ps, sem, as_f32, seq_dram, ident, cond_cols, bias_cols, neg_half,
        w1, w2, b2, x1_dram, gate_dram, out):
    RING = 3
    with ExitStack() as st:
        w1_t = [sb(st, f"w1_t{i}", [P, KD, DFF], f32r) for i in range(2)]
        w2_t = [sb(st, f"w2_t{i}", [P, NJ, D], f32r) for i in range(2)]
        w1_in = [sb(st, f"w1_in{i}", [P, D]) for i in range(RING)]
        w2_in = [sb(st, f"w2_in{i}", [P, KD, P]) for i in range(RING)]
        xb = sb(st, "xb", [P, TT, D])
        stats = sb(st, "stats2", [P, TT, 6])
        mean_var = sb(st, "mean_var2", [P, TT, 2])
        var_eps = sb(st, "var_eps2", [P, TT])
        rstd = sb(st, "rstd2", [P, TT])
        shift_col = sb(st, "shift_col2", [P, TT])
        cond_now = sb(st, "cond_now2", [P, NC])
        h_full = [sb(st, f"h2_full{i}", [P, N]) for i in range(2)]
        h = [sb(st, f"h2_{i}", [P, KD, N], f32r) for i in range(2)]
        gelu_full = [sb(st, f"gelu_full{i}", [P, N]) for i in range(2)]
        hidden = [[sb(st, f"hidden{s}{i}", [P, N], f32r) for i in range(2)] for s in range(2)]
        resid = sb(st, "resid2", [P, TT, D])
        y = sb(st, "y", [P, TT, D])
        gate_now = sb(st, "gate_now2", [P, D])
        b2_rows = sb(st, "b2_rows", [P, D])

        acc = [ps(st, f"acc{i}", [P, D]) for i in range(TT)]
        up = [ps(st, f"up{i}", [P, N]) for i in range(2)]
        turn = [ps(st, f"turn{i}", [P, N]) for i in range(2)]

        w_loaded = [sem(f"w_ring{i}") for i in range(RING)]
        x_loaded, stats_done, moments_done, eps_added = sem("x_loaded2"), sem("stats_done2"), sem("moments_done2"), sem("eps_added2")
        rstd_ready, shift_ready, normed, cond_copied = sem("rstd_ready2"), sem("shift_ready2"), sem("normed2"), sem("cond_copied2")
        turned, turn_free, h_ready, h_hi, h_split = sem("turned"), sem("turn_free"), sem("h_ready2"), sem("h_hi2"), sem("h_split2")
        w_turned, w_hi, w_split = sem("w_turned2"), sem("w_hi2"), sem("w_split2")
        up_ready, gelu_done, hid_hi, hid_split, down_done = sem("up_ready"), sem("gelu_done"), sem("hid_hi"), sem("hid_split"), sem("down_done")
        acc_ready, acc_taken, y_gated, y_added = sem("acc_ready"), sem("acc_taken"), sem("y_gated"), sem("y_added")
        b2_loaded, gate_loaded, resid_loaded, out_stored = sem("b2_loaded"), sem("gate_loaded2"), sem("resid_loaded2"), sem("out_stored")

        def sequences(eng, body):
            body(0, True, True)
            with eng.Fori(1, B - 1) as b:
                body(b, False, True)
            body(B - 1, False, False)

        with nc.Block() as block:
            @block.sync
            def _(sp):
                def body(b, is_first, has_next):
                    if is_first:
                        sp.dma_start(xb[:, :, :], seq_dram(x1_dram, b)).then_inc(x_loaded, 16)
                        sp.dma_start(b2_rows[:, :], b2.rearrange("(a d) -> a d", a=1).partition_broadcast(P).rearrange("p a d -> p (a d)")).then_inc(b2_loaded, 16)
                        for j in range(NJ):
                            if j == RING:
                                load_next(b)
                            if j >= RING:
                                sp.wait_ge(w_turned, 2 * (j - RING) + 2)
                            sp.dma_start(w1_in[j % RING][:, :], w1[j * P:j * P + P, :]).then_inc(w_loaded[j % RING], 16)
                            sp.dma_start(w2_in[j % RING][:, :, :],
                                         w2[:, j * P:j * P + P].rearrange("(o p) i -> p o i", p=P)).then_inc(w_loaded[j % RING], 16)
                    elif has_next:
                        load_next(b)
                    if not is_first:
                        store(b - 1)
                    sp.dma_start(gate_now[:, :], gate_dram[bass.ds(b, 1), 1, :].partition_broadcast(P).rearrange("p a d -> p (a d)")).then_inc(gate_loaded, 16)
                    sp.dma_start(resid[:, :, :], seq_dram(x1_dram, b)).then_inc(resid_loaded, 16)
                    if not has_next:
                        store(b)

                def load_next(b):
                    sp.wait_ge(turned, b * KD + KD)
                    sp.dma_start(xb[:, :, :], seq_dram(x1_dram, b + 1)).then_inc(x_loaded, 16)

                def store(b):
                    sp.wait_ge(y_added, b * TT + TT)
                    sp.dma_start(seq_dram(out, b), y[:, :, :]).then_inc(out_stored, 16)
                    sp.wait_ge(out_stored, b * 16 + 16)

                sequences(sp, body)

            @block.gpsimd
            def _(pool):
                def rstd_of(b):
                    pool.wait_ge(eps_added, b + 1)
                    nc.gpsimd.tensor_tensor(rstd[:, :], var_eps[:, :], neg_half[:, :], ALU.pow).then_inc(rstd_ready, 1)

                def body(b, is_first, has_next):
                    if is_first:
                        rstd_of(0)
                    if has_next:
                        rstd_of(b + 1)
                    pool.wait_ge(gate_loaded, b * 16 + 16)
                    pool.wait_ge(resid_loaded, b * 16 + 16)
                    for tt in range(TT):
                        n = b * TT + (tt + 1)
                        pool.wait_ge(acc_taken, n)
                        nc.gpsimd.tensor_tensor(y[:, tt, :], y[:, tt, :], gate_now[:, :], ALU.mult).then_inc(y_gated, 1)
                        pool.wait_ge(y_gated, n)
                        nc.gpsimd.tensor_tensor(y[:, tt, :], y[:, tt, :], resid[:, tt, :], ALU.add).then_inc(y_added, 1)

                sequences(pool, body)

            @block.scalar
            def _(act):
                def norm(b):
                    act.wait_ge(shift_ready, b + 1)
                    for tt in range(TT):
                        nc.scalar.activation(xb[:, tt, :], xb[:, tt, :], ACT.Identity, scale=rstd[:, tt:tt + 1],
                                             bias=shift_col[:, tt:tt + 1]).then_inc(normed, 1)

                def modulate(b, kt, is_first=False):
                    if kt == 0:
                        act.wait_ge(cond_copied, b + 1)
                    act.wait_ge(turned, b * KD + (kt + 1))
                    if not (is_first and kt < 2):
                        act.wait_ge(h_split, b * KD + (kt - 1))
                    nc.scalar.activation(h_full[kt % 2][:, :], turn[kt % 2][:, :], ACT.Identity,
                                         scale=cond_now[:, SC2 + kt:SC2 + kt + 1],
                                         bias=cond_now[:, SH2 + kt:SH2 + kt + 1]).then_inc(h_ready, 1)

                def weights_high(j):
                    act.wait_ge(w_turned, 2 * j + 1)
                    nc.scalar.activation(w1_t[0][:, :, j * P:j * P + P], turn[0][:, :].rearrange("p (k n) -> p k n", k=KD),
                                         ACT.Copy).then_inc(w_hi, 1)
                    act.wait_ge(w_turned, 2 * j + 2)
                    nc.scalar.activation(w2_t[0][:, j, :], turn[1][:, :], ACT.Copy).then_inc(w_hi, 1)

                def body(b, is_first, has_next):
                    if is_first:
                        norm(0)
                        for kt in range(KD):
                            modulate(0, kt, is_first=True)
                        weights_high(0)
                    for j in range(NJ):
                        t = b * NJ + j
                        if is_first and j + 1 < NJ:
                            weights_high(j + 1)
                        act.wait_ge(up_ready, t + 1)
                        if not (is_first and j < 2):
                            act.wait_ge(hid_split, t - 1)
                        nc.scalar.activation(gelu_full[j % 2][:, :], up[j % 2][:, :], ACT.Gelu,
                                             bias=bias_cols[:, NC + j:NC + j + 1]).then_inc(gelu_done, 1)
                        if has_next and j == 9:
                            norm(b + 1)
                    if has_next:
                        for kt in range(KD):
                            modulate(b + 1, kt)

                sequences(act, body)

            @block.vector
            def _(dve):
                def tile_stats(b):
                    nc.vector.tensor_copy(cond_now[:, :], cond_cols[:, bass.ds(b, 1), :].rearrange("p a j -> p (a j)")).then_inc(cond_copied, 1)
                    dve.wait_ge(x_loaded, b * 16 + 16)
                    for tt in range(TT):
                        nc.vector.bn_stats(stats[:, tt, :], xb[:, tt, :]).then_inc(stats_done, 1)

                def moments(b):
                    for tt in range(TT):
                        nc.vector.bn_aggr(mean_var[:, tt, :], stats[:, tt, :]).then_inc(moments_done, 1)
                    dve.wait_ge(moments_done, b * TT + TT)
                    nc.vector.tensor_scalar(var_eps[:, :], mean_var[:, :, 1], EPS, None, ALU.add).then_inc(eps_added, 1)

                def shift_of(b):
                    dve.wait_ge(rstd_ready, b + 1)
                    nc.vector.scalar_tensor_tensor(out=shift_col[:, :], in0=mean_var[:, :, 0], scalar=-1.0,
                                                   in1=rstd[:, :], op0=ALU.mult, op1=ALU.mult).then_inc(shift_ready, 1)

                def split_h(b, kt):
                    n = b * KD + (kt + 1)
                    dve.wait_ge(h_ready, n)
                    nc.vector.tensor_copy(h[0][:, kt, :], h_full[kt % 2][:, :]).then_inc(h_hi, 1)
                    dve.wait_ge(h_hi, n)
                    nc.vector.tensor_tensor(h[1][:, kt, :], h_full[kt % 2][:, :], as_f32(h[0][:, kt, :]),
                                            ALU.subtract).then_inc(h_split, 1)

                def weights_low(j):
                    dve.wait_ge(w_hi, 2 * j + 1)
                    nc.vector.tensor_tensor(w1_t[1][:, :, j * P:j * P + P], turn[0][:, :].rearrange("p (k n) -> p k n", k=KD),
                                            as_f32(w1_t[0][:, :, j * P:j * P + P]), ALU.subtract).then_inc(w_split, 1)
                    dve.wait_ge(w_hi, 2 * j + 2)
                    nc.vector.tensor_tensor(w2_t[1][:, j, :], turn[1][:, :], as_f32(w2_t[0][:, j, :]),
                                            ALU.subtract).then_inc(w_split, 1)

                def split_hidden(b, j, is_first):
                    n = b * NJ + (j + 1)
                    dve.wait_ge(gelu_done, n)
                    if j >= 2:
                        dve.wait_ge(down_done, b * (NJ - 1) + (j - 1))
                    elif not is_first:
                        dve.wait_ge(*((down_done, b * (NJ - 1)) if j == 0 else (acc_ready, b * TT)))
                    nc.vector.tensor_copy(hidden[j % 2][0][:, :], gelu_full[j % 2][:, :]).then_inc(hid_hi, 1)
                    dve.wait_ge(hid_hi, n)
                    nc.vector.tensor_tensor(hidden[j % 2][1][:, :], gelu_full[j % 2][:, :], as_f32(hidden[j % 2][0][:, :]),
                                            ALU.subtract).then_inc(hid_split, 1)

                def take_acc(b, is_first):
                    if not is_first:
                        dve.wait_ge(out_stored, b * 16)
                    for tt in range(TT):
                        dve.wait_ge(acc_ready, b * TT + (tt + 1))
                        nc.vector.tensor_tensor(y[:, tt, :], acc[tt][:, :], b2_rows[:, :], ALU.add).then_inc(acc_taken, 1)

                def body(b, is_first, has_next):
                    if is_first:
                        tile_stats(0)
                        dve.wait_ge(stats_done, TT)
                        moments(0)
                        shift_of(0)
                        for kt in range(KD):
                            split_h(0, kt)
                        weights_low(0)
                        dve.wait_ge(b2_loaded, 16)
                    for j in range(NJ):
                        if is_first and j + 1 < NJ:
                            weights_low(j + 1)
                        if has_next and j == 6:
                            dve.wait_ge(stats_done, b * TT + 2 * TT)
                        split_hidden(b, j, is_first)
                        if has_next and j == 5:
                            tile_stats(b + 1)
                        if has_next and j == 6:
                            moments(b + 1)
                        if has_next and j == 8:
                            shift_of(b + 1)
                    if has_next:
                        dve.wait_ge(up_ready, b * NJ + NJ)
                        for kt in range(KD):
                            split_h(b + 1, kt)
                    take_acc(b, is_first)

                sequences(dve, body)

            @block.tensor
            def _(pe):
                PASSES = ((0, 0), (0, 1), (1, 0))

                def turn_x(b, kt, is_first=False):
                    if is_first:
                        if kt >= 2:
                            pe.wait_ge(h_ready, kt - 1)
                    elif kt >= 2:
                        pe.wait_ge(h_ready, b * KD + (kt - 1))
                    else:
                        pe.wait_ge(h_ready, b * KD)
                        pe.wait_ge(w_split, 2 * NJ)
                    for tt in range(TT):
                        if kt == 0:
                            pe.wait_ge(normed, b * TT + (tt + 1))
                        last = nc.tensor.transpose(turn[kt % 2][:, tt * P:tt * P + P], xb[:, tt, kt * P:kt * P + P], ident[:, :])
                    last.then_inc(turned, 1)

                def turn_weights(j):
                    pe.wait_ge(w_loaded[j % RING], 32 * (j // RING) + 32)
                    if j == 0:
                        pe.wait_ge(h_ready, KD)
                    else:
                        pe.wait_ge(w_split, 2 * j - 1)
                    for kt in range(KD):
                        last = nc.tensor.transpose(turn[0][:, kt * P:kt * P + P], w1_in[j % RING][:, kt * P:kt * P + P], ident[:, :])
                    last.then_inc(w_turned, 1)
                    if j > 0:
                        pe.wait_ge(w_split, 2 * j)
                    for o in range(KD):
                        last = nc.tensor.transpose(turn[1][:, o * P:o * P + P], w2_in[j % RING][:, o, :], ident[:, :])
                    last.then_inc(w_turned, 1)

                def up_product(b, j, is_first):
                    if j == 0:
                        pe.wait_ge(h_split, b * KD + KD)
                    if is_first:
                        pe.wait_ge(w_split, 2 * j + 2)
                    if not (is_first and j < 2):
                        pe.wait_ge(gelu_done, b * NJ + (j - 1))
                    for kt in range(KD):
                        for n, (i, k) in enumerate(PASSES):
                            last = nc.tensor.matmul(up[j % 2][:, :], w1_t[i][:, kt, j * P:j * P + P], h[k][:, kt, :],
                                                    start=(kt == 0 and n == 0), stop=(kt == KD - 1 and n == 2))
                    last.then_inc(up_ready, 1)

                def down_product(b, j, is_first):
                    pe.wait_ge(hid_split, b * NJ + (j + 1))
                    for tt in range(TT):
                        if j == 0 and not is_first:
                            pe.wait_ge(acc_taken, b * TT - TT + (tt + 1))
                        for n, (i, k) in enumerate(PASSES):
                            last = nc.tensor.matmul(acc[tt][:, :], hidden[j % 2][i][:, tt * P:tt * P + P], w2_t[k][:, j, :],
                                                    start=(j == 0 and n == 0), stop=(j == NJ - 1 and n == 2))
                        if j == NJ - 1:
                            last.then_inc(acc_ready, 1)
                    if j < NJ - 1:
                        last.then_inc(down_done, 1)

                def body(b, is_first, has_next):
                    if is_first:
                        for kt in range(KD):
                            turn_x(0, kt, is_first=True)
                        turn_weights(0)
                    for j in range(NJ):
                        if is_first and j + 1 < NJ:
                            turn_weights(j + 1)
                        up_product(b, j, is_first)
                        if j >= 1:
                            down_product(b, j - 1, is_first)
                        if has_next and j == NJ - 2:
                            turn_x(b + 1, 0)
                            turn_x(b + 1, 1)
                    down_product(b, NJ - 1, is_first)
                    if has_next:
                        turn_x(b + 1, 2)
                        turn_x(b + 1, 3)

                sequences(pe, body)


_INS = ["x", "cond_1024", "L0_cond_wq", "L0_cond_wk", "L0_cond_wv", "L0_cond_wo", "L0_cond_w1", "L0_cond_b1",
        "L0_cond_w2", "L0_cond_b2", "L0_cond_wc", "L0_cond_bc"]


def kernel(**inputs):
    import numpy as _np
    import concourse.bacc as _bacc
    from concourse import mybir as _mybir
    from concourse.bass_utils import run_bass_kernel_spmd as _run

    nc = _bacc.Bacc("TRN2", target_bir_lowering=False, num_devices=1)
    arrays, args = {}, []
    for name in _INS:
        a = _np.ascontiguousarray(inputs[name])
        arrays[f"in_{name}_dram"] = a
        args.append(nc.dram_tensor(f"in_{name}_dram", a.shape, _mybir.dt.from_np(a.dtype), kind="ExternalInput").ap())
    out = nc.dram_tensor("out_0_dram", (B, N, D), _mybir.dt.float32, kind="ExternalOutput").ap()
    layer_kernel(nc, *args, out)
    r = _run(nc, [arrays], core_ids=[0])
    return r.results[0]["out_0_dram"]
```

```python
import concourse.bass as bass
from concourse import mybir
from contextlib import ExitStack


P = 128
B, N, D = 8, 512, 512
HKV, R, HD = 4, 4, 32
DFF = 2048
TT = N // P
KD = D // P
NJ = DFF // P
RING = 3
NC = 4 * KD
SH1, SC1, SH2, SC2 = (i * KD for i in range(4))
EPS = 1e-5
SCORE_SCALE = 1.0 / float(HD) ** 0.5
STACK = 3 * HD
SHIFT = STACK + 2

FILL = {(0, 0): ["VT", "Q2"], (0, 3): ["Q3"], (1, 0): ["O0"], (1, 1): ["O1"], (1, 2): ["O2"], (1, 3): ["T0", "T1", "O3"],
        (2, 0): ["T2", "T3"], (2, 1): ["K"], (2, 2): ["Q0"], (2, 3): ["Q1"], (3, 3): ["V"]}
ROWS_IN_SLOT = [[5, 7, 4, 0], [6, 6, 4, 0], [6, 6, 4, 0], [5, 7, 4, 0]]
FIRST_ROW = [[sum(n[:i]) for i in range(TT)] for n in ROWS_IN_SLOT]
TAKER = {"T": "act", "V": "act", "K": "dve", "Q": "dve", "O": "dve"}


def fill(g, kt, has_last, has_next):
    return [n for n in FILL.get((g, kt), [])
            if (has_last or n[0] != "O") and (has_next or n not in ("K", "Q0", "Q1", "V"))]


class Units:

    def __init__(self, order, base):
        self.at = {name: i for i, name in enumerate(order)}
        self.order, self.base = order, base

    def bank(self, name):
        return self.at[name] % 2

    def ready(self, name):
        return self.base["all"] + (self.at[name] + 1)

    def taken(self, name):
        who = TAKER[name[0]]
        mine = [n for n in self.order if TAKER[n[0]] == who]
        return self.base[who] + (mine.index(name) + 1)

    def after(self):
        return {k: self.base[k] + n for k, n in sizes(self.order).items()}


def sizes(order):
    return {"all": len(order), "act": sum(TAKER[n[0]] == "act" for n in order),
            "dve": sum(TAKER[n[0]] == "dve" for n in order)}


def seq_order(has_last, has_next):
    return [n for g in range(HKV) for kt in range(TT) for n in fill(g, kt, has_last, has_next)]


def before_units():
    return Units(["T0", "T1", "T2", "T3", "K", "Q0", "Q1", "V"], {"all": 0, "act": 0, "dve": 0})


def seq_units(b, has_last, has_next):
    ahead = before_units().after()
    if has_last:
        ahead = Units(seq_order(False, True), ahead).after()
        step = sizes(seq_order(True, True))
        ahead = {k: (b - 1) * step[k] + ahead[k] for k in ahead}
    return Units(seq_order(has_last, has_next), ahead)


def after_units():
    return Units(["O0", "O1", "O2", "O3"], seq_units(B - 1, True, False).after())


ROWS = R * TT


def row_no(b, g, i):
    return b * (HKV * (ROWS + 1)) + (g * (ROWS + 1) + i)


def layer_kernel(nc, x, cond, wq, wk, wv, wo, w1, b1, w2, b2, wc, bc, out):
    f32, f32r = mybir.dt.float32, mybir.dt.float32r
    ALU, ACT, AX = mybir.AluOpType, mybir.ActivationFunctionType, mybir.AxisListType

    x1_dram = nc.dram_tensor("x1_scratch", (B, N, D), f32, kind="Internal").ap()
    gate_dram = nc.dram_tensor("gate_scratch", (B, 2, D), f32, kind="Internal").ap()

    def seq_dram(t, b):
        return t[bass.ds(b, 1), :, :].rearrange("a (t p) d -> p (a t) d", p=P)

    def as_f32(ap):
        return ap.bitcast(f32)

    with ExitStack() as ctx:
        def sb(stack, name, shape, dt=f32):
            return stack.enter_context(nc.sbuf_tensor(name, shape, dt))

        def ps(stack, name, shape, dt=f32):
            return stack.enter_context(nc.psum_tensor(name, shape, dt))

        def sem(name):
            return ctx.enter_context(nc.semaphore(name))

        ident = sb(ctx, "ident", [P, P])
        cond_cols = sb(ctx, "cond_cols", [P, B, NC])
        bias_cols = sb(ctx, "bias_cols", [P, NJ])
        neg_half = sb(ctx, "neg_half", [P, TT])
        xa = sb(ctx, "xa", [P, TT, D])
        stats = sb(ctx, "stats", [P, TT, 6])
        mean_var = sb(ctx, "mean_var", [P, TT, 2])
        var_eps = sb(ctx, "var_eps", [P, TT])
        rstd = sb(ctx, "rstd", [P, TT])
        shift_col = sb(ctx, "shift_col", [P, TT])
        cond_now = sb(ctx, "cond_now", [P, NC])
        h_full = [sb(ctx, f"h_full{i}", [P, N]) for i in range(2)]
        h = [sb(ctx, f"h{i}", [P, KD, N], f32r) for i in range(2)]
        spare = [[sb(ctx, f"spare{i}{j}", [P, N], f32r) for j in range(2)] for i in range(RING)]
        resid = sb(ctx, "resid", [P, TT, D])
        gate_now = sb(ctx, "gate_now", [P, D])
        x1_stored = sem("x1_stored")
        w_loaded = [sem(f"w_ring{i}") for i in range(RING)]

        def load_weights(sp, j):
            sp.dma_start(as_f32(spare[j % RING][0][:, :]), w1[j * P:j * P + P, :]).then_inc(w_loaded[j % RING], 16)
            sp.dma_start(as_f32(spare[j % RING][1][:, :]).rearrange("p (o i) -> p o i", o=KD),
                         w2[:, j * P:j * P + P].rearrange("(o p) i -> p o i", p=P)).then_inc(w_loaded[j % RING], 16)

        norm_bufs = (xa, stats, mean_var, var_eps, rstd, shift_col, cond_now, h_full, h)

        attn_ctx = ExitStack()
        with attn_ctx:
            wq_t = [sb(attn_ctx, f"wq_t{i}", [P, KD, D], f32r) for i in range(2)]
            wk_t = [sb(attn_ctx, f"wk_t{i}", [P, KD, P], f32r) for i in range(2)]
            wv_t = [sb(attn_ctx, f"wv_t{i}", [P, KD, P], f32r) for i in range(2)]
            wo_t = [sb(attn_ctx, f"wo_t{i}", [P, KD, D], f32r) for i in range(2)]

            norm_sems = tuple(sem(n) for n in ("x_loaded", "stats_done", "moments_done", "eps_added", "rstd_ready",
                                               "shift_ready", "normed"))

            prologue(nc, f32, f32r, ALU, ACT, sb, ps, sem, seq_dram, ident, cond_cols, bias_cols, neg_half, norm_bufs,
                     norm_sems, wq_t, wk_t, wv_t, wo_t, x, cond, wq, wk, wv, wo, b1, wc, bc, gate_dram)
            attention(nc, f32, f32r, ALU, ACT, AX, sb, ps, sem, as_f32, seq_dram, ident, cond_cols, neg_half, norm_bufs,
                      norm_sems, spare, resid, gate_now, x1_stored, load_weights, wq_t, wk_t, wv_t, wo_t, x, x1_dram, gate_dram)
        mlp(nc, f32, f32r, ALU, ACT, sb, ps, sem, as_f32, seq_dram, ident, cond_cols, bias_cols, neg_half, norm_bufs,
            spare, resid, gate_now, x1_stored, w_loaded, load_weights, b2, x1_dram, gate_dram, out)


def prologue(nc, f32, f32r, ALU, ACT, sb, ps, sem, seq_dram, ident, cond_cols, bias_cols, neg_half, norm_bufs, norm_sems,
             wq_t, wk_t, wv_t, wo_t, x, cond, wq, wk, wv, wo, b1, wc, bc, gate_dram):
    xa, stats, mean_var, var_eps, rstd, shift_col, _, _, _ = norm_bufs
    x_loaded, stats_done, moments_done, eps_added, rstd_ready, shift_ready, normed = norm_sems
    RAW, LAG = 4, 2
    parts = [[(f"c{i}", kt) for kt in range(KD)] for i in range(6)]
    units = (parts[0] + parts[1] + [("q", kt) for kt in range(KD)] + [("k", 0), ("v", 0)]
             + parts[2] + [("o", kt) for kt in range(KD)] + parts[3] + parts[4] + parts[5])
    products = [u for u, (which, _) in enumerate(units) if which[0] == "c"]
    TURNED_BACK = [0, 1, 3, 4]
    with ExitStack() as st:
        c_row = sb(st, "c_row", [B, D])
        silu_row = sb(st, "silu_row", [B, D])
        silu_t = [sb(st, f"silu_t{i}", [P, KD * B], f32r) for i in range(2)]
        b1_rows = sb(st, "b1_rows", [NJ, P])
        bc_rows = sb(st, "bc_rows", [B, 6 * D])
        cond_rows = sb(st, "cond_rows", [B, 6, D])
        raw = {"q": sb(st, "wq_in", [P, KD, D]), "k": sb(st, "wk_in", [P, 1, D]),
               "v": sb(st, "wv_in", [P, 1, D]), "o": sb(st, "wo_in", [P, KD, D])}
        for i in range(6):
            raw[f"c{i}"] = sb(st, f"wc_in{i}", [P, KD, D])
        wc_t = [[sb(st, f"wc_t{s}{i}", [P, D], f32r) for i in range(2)] for s in range(RAW)]
        w_bank = [ps(st, f"w_bank{i}", [P, D]) for i in range(RAW)]
        cond_bank = [ps(st, f"cond_bank{i}", [P, D]) for i in range(2)]
        small_bank = ps(st, "small_bank", [P, D])
        col_bank = ps(st, "col_bank", [P, D])

        ident_zero, ident_ready, half_ready = sem("ident_zero"), sem("ident_ready"), sem("half_ready")
        c_loaded, b1_loaded, bc_loaded = sem("c_loaded"), sem("b1_loaded"), sem("bc_loaded")
        raw_loaded = {n: sem(f"raw_loaded_{n}") for n in raw}
        silu_done, silu_turned, silu_hi, silu_split = sem("silu_done"), sem("silu_turned"), sem("silu_hi"), sem("silu_split")
        b1_turned = sem("b1_turned")
        w_turned, w_hi, w_split = sem("w_turned"), sem("w_hi"), sem("w_split")
        multiplied, part_ready, part_biased = sem("multiplied"), sem("part_ready"), sem("part_biased")
        cols_turned, cols_taken, b1_taken, gates_stored = sem("cols_turned"), sem("cols_taken"), sem("b1_taken"), sem("gates_stored")
        w_dst = {"q": wq_t, "k": wk_t, "v": wv_t, "o": wo_t}

        def unit_dst(u, half):
            which, kt = units[u]
            if which[0] == "c":
                return wc_t[products.index(u) % RAW][half][:, :]
            if which in "qo":
                return w_dst[which][half][:, kt, :]
            return w_dst[which][half][:, :, :].rearrange("p k n -> p (k n)")

        with nc.Block() as block:
            @block.sync
            def _(sp):
                def load(name, w):
                    sp.dma_start(raw[name][:, :, :], w.rearrange("(o p) i -> p o i", p=P)).then_inc(raw_loaded[name], 16)

                def load_part(i):
                    load(f"c{i}", wc[D * i:D * i + D, :])

                sp.dma_start(c_row[:, :], cond).then_inc(c_loaded, 16)
                load_part(0)
                load_part(1)
                sp.dma_start(bc_rows[:, :], bc.rearrange("(a d) -> a d", a=1).partition_broadcast(B)
                             .rearrange("p a d -> p (a d)")).then_inc(bc_loaded, 16)
                load("q", wq)
                load("k", wk)
                load("v", wv)
                sp.dma_start(xa[:, :, :], seq_dram(x, 0)).then_inc(x_loaded, 16)
                load_part(2)
                load("o", wo)
                load_part(3)
                load_part(4)
                load_part(5)
                sp.dma_start(b1_rows[:, :], b1.rearrange("(j p) -> j p", p=P)).then_inc(b1_loaded, 16)
                sp.wait_ge(part_biased, 3)
                sp.dma_start(gate_dram[:, 0, :], cond_rows[:, 2, :]).then_inc(gates_stored, 16)
                sp.wait_ge(part_biased, 6)
                sp.dma_start(gate_dram[:, 1, :], cond_rows[:, 5, :]).then_inc(gates_stored, 16)
                sp.wait_ge(gates_stored, 32)

            @block.gpsimd
            def _(pool):
                nc.gpsimd.memset(ident[:, :], 0.0).then_inc(ident_zero, 1)
                pool.wait_ge(ident_zero, 1)
                nc.gpsimd.affine_select(out=ident[:, :], in_=ident[:, :], compare_op=ALU.not_equal, fill=1.0,
                                        base=0, pattern=[[-1, P]], channel_multiplier=1).then_inc(ident_ready, 1)
                nc.gpsimd.memset(neg_half[:, :], -0.5).then_inc(half_ready, 1)
                pool.wait_ge(half_ready, 1)
                pool.wait_ge(eps_added, 1)
                nc.gpsimd.tensor_tensor(rstd[:, :], var_eps[:, :], neg_half[:, :], ALU.pow).then_inc(rstd_ready, 1)

            @block.scalar
            def _(act):
                act.wait_ge(c_loaded, 16)
                nc.scalar.activation(silu_row[:, :], c_row[:, :], ACT.Silu).then_inc(silu_done, 1)
                nc.scalar.preload_act_table_set("natural_log_exp_and_others")
                act.wait_ge(silu_turned, 1)
                nc.scalar.activation(silu_t[0][:, :], small_bank[:, 0:KD * B], ACT.Copy).then_inc(silu_hi, 1)
                for u in range(len(units)):
                    act.wait_ge(w_turned, u + 1)
                    if u in products and products.index(u) >= RAW:
                        i, kt = divmod(products.index(u) - RAW, KD)
                        act.wait_ge(*((multiplied, i * (KD - 1) + (kt + 1)) if kt < KD - 1 else (part_ready, i + 1)))
                    nc.scalar.activation(unit_dst(u, 0), w_bank[u % RAW][:, :], ACT.Copy).then_inc(w_hi, 1)
                    if units[u] == ("c2", 3):
                        act.wait_ge(shift_ready, 1)
                        for tt in range(TT):
                            nc.scalar.activation(xa[:, tt, :], xa[:, tt, :], ACT.Identity, scale=rstd[:, tt:tt + 1],
                                                 bias=shift_col[:, tt:tt + 1]).then_inc(normed, 1)

            @block.vector
            def _(dve):
                def add_bias(i):
                    dve.wait_ge(part_ready, i + 1)
                    if i == 0:
                        dve.wait_ge(bc_loaded, 16)
                    nc.vector.tensor_tensor(cond_rows[:, i, :], cond_bank[i % 2][0:B, :], bc_rows[:, i * D:i * D + D],
                                            ALU.add).then_inc(part_biased, 1)

                def take_columns(i):
                    n = TURNED_BACK.index(i)
                    dve.wait_ge(cols_turned, n + 1)
                    nc.vector.tensor_scalar(cond_cols[:, :, n * KD:n * KD + KD],
                                            col_bank[:, n * KD * B:(n + 1) * KD * B].rearrange("p (k b) -> p b k", k=KD),
                                            1.0 if i in (1, 4) else 0.0, None, ALU.add).then_inc(cols_taken, 1)

                dve.wait_ge(silu_hi, 1)
                nc.vector.tensor_tensor(silu_t[1][:, :], small_bank[:, 0:KD * B], silu_t[0][:, :].bitcast(f32),
                                        ALU.subtract).then_inc(silu_split, 1)
                biased, turned_back = 0, []
                for u in range(len(units)):
                    dve.wait_ge(w_hi, u + 1)
                    nc.vector.tensor_tensor(unit_dst(u, 1), w_bank[u % RAW][:, :], unit_dst(u, 0).bitcast(f32),
                                            ALU.subtract).then_inc(w_split, 1)
                    if turned_back and u >= turned_back[0][1]:
                        take_columns(turned_back.pop(0)[0])
                    if biased < 6 and u >= units.index((f"c{biased}", KD - 1)) + LAG + 1:
                        add_bias(biased)
                        if biased in TURNED_BACK:
                            turned_back.append((biased, u + 2))
                        biased += 1
                    if units[u] == ("c2", 0):
                        dve.wait_ge(x_loaded, 16)
                        for tt in range(TT):
                            nc.vector.bn_stats(stats[:, tt, :], xa[:, tt, :]).then_inc(stats_done, 1)
                        dve.wait_ge(stats_done, TT)
                        for tt in range(TT):
                            nc.vector.bn_aggr(mean_var[:, tt, :], stats[:, tt, :]).then_inc(moments_done, 1)
                        dve.wait_ge(moments_done, TT)
                        nc.vector.tensor_scalar(var_eps[:, :], mean_var[:, :, 1], EPS, None, ALU.add).then_inc(eps_added, 1)
                    if units[u] == ("c2", 2):
                        dve.wait_ge(rstd_ready, 1)
                        nc.vector.scalar_tensor_tensor(out=shift_col[:, :], in0=mean_var[:, :, 0], scalar=-1.0,
                                                       in1=rstd[:, :], op0=ALU.mult, op1=ALU.mult).then_inc(shift_ready, 1)
                for i in range(biased, 6):
                    add_bias(i)
                for i, _ in turned_back:
                    take_columns(i)
                dve.wait_ge(b1_turned, 1)
                nc.vector.tensor_copy(bias_cols[:, :], small_bank[:, KD * B:KD * B + NJ]).then_inc(b1_taken, 1)

            @block.tensor
            def _(pe):
                def multiply(u):
                    i, kt = int(units[u][0][1]), units[u][1]
                    n = products.index(u)
                    pe.wait_ge(w_split, u + 1)
                    if kt == 0 and i >= 2:
                        pe.wait_ge(part_biased, i - 1)
                    for m, (a, b) in enumerate(((0, 0), (1, 0), (0, 1))):
                        last = nc.tensor.matmul(cond_bank[i % 2][0:B, :], silu_t[a][:, kt * B:kt * B + B],
                                                wc_t[n % RAW][b][:, :], start=(kt == 0 and m == 0),
                                                stop=(kt == KD - 1 and m == 2))
                    last.then_inc(multiplied if kt < KD - 1 else part_ready, 1)

                def turn_columns(i):
                    n = TURNED_BACK.index(i)
                    pe.wait_ge(part_biased, i + 1)
                    for kt in range(KD):
                        last = nc.tensor.transpose(col_bank[:, (n * KD + kt) * B:(n * KD + kt + 1) * B],
                                                   cond_rows[:, i, kt * P:kt * P + P], ident[0:B, 0:B])
                    last.then_inc(cols_turned, 1)

                pe.wait_ge(ident_ready, 1)
                pe.wait_ge(silu_done, 1)
                for kt in range(KD):
                    last = nc.tensor.transpose(small_bank[:, kt * B:kt * B + B], silu_row[:, kt * P:kt * P + P],
                                               ident[0:B, 0:B])
                last.then_inc(silu_turned, 1)
                turned_back = []
                for u in range(len(units) + LAG):
                    if u < len(units):
                        which, kt = units[u]
                        pe.wait_ge(raw_loaded[which], 16)
                        if u >= RAW:
                            pe.wait_ge(w_split, u - (RAW - 1))
                        for i in range(KD):
                            src = (raw[which][:, 0, i * P:i * P + P] if which in "kv"
                                   else raw[which][:, i, kt * P:kt * P + P])
                            last = nc.tensor.transpose(w_bank[u % RAW][:, i * P:i * P + P], src, ident[:, :])
                        last.then_inc(w_turned, 1)
                    if u == LAG:
                        pe.wait_ge(silu_split, 1)
                    if u - LAG in products:
                        multiply(u - LAG)
                        if units[u - LAG][1] == KD - 1 and int(units[u - LAG][0][1]) in TURNED_BACK:
                            turned_back.append((int(units[u - LAG][0][1]), u + 3))
                    if turned_back and u >= turned_back[0][1]:
                        turn_columns(turned_back.pop(0)[0])
                for i, _ in turned_back:
                    turn_columns(i)
                pe.wait_ge(b1_loaded, 16)
                nc.tensor.transpose(small_bank[:, KD * B:KD * B + NJ], b1_rows[:, :], ident[0:NJ, 0:NJ]).then_inc(b1_turned, 1)


def attention(nc, f32, f32r, ALU, ACT, AX, sb, ps, sem, as_f32, seq_dram, ident, cond_cols, neg_half, norm_bufs, norm_sems,
              spare, resid, gate_now, x1_stored, load_weights, wq_t, wk_t, wv_t, wo_t, x, x1_dram, gate_dram):
    xa, stats, mean_var, var_eps, rstd, shift_col, cond_now, h_full, h = norm_bufs
    x_loaded, stats_done, moments_done, eps_added, rstd_ready, shift_ready, normed = norm_sems
    with ExitStack() as st:
        k_part, q_part = spare[0], spare[1:]
        v_full = sb(st, "v_full", [P, N])
        v = sb(st, "v", [P, TT, P])
        k_stack = sb(st, "k_stack", [P, HKV, N], f32r)
        q_stack = sb(st, "q_stack", [P, HKV, R, N], f32r)
        neg_max = sb(st, "neg_max", [P, 2, ROWS])
        max_row = [sb(st, f"max_row{i}", [ROWS, P], f32r) for i in range(2)]
        probs = [sb(st, f"probs{i}", [P, R, N]) for i in range(TT)]
        probs_sum = sb(st, "probs_sum", [P, R, N])
        ones = sb(st, "ones", [P, HD])
        inverse = sb(st, "inverse", [P, N])
        refined = sb(st, "refined", [P, N])
        attn_raw = sb(st, "attn_raw", [P, N])
        attn_full = sb(st, "attn_full", [P, N])
        attn = [sb(st, f"attn{i}", [P, HKV, N], f32r) for i in range(2)]
        gated = [sb(st, f"gated{i}", [P, D]) for i in range(2)]

        key_bank = [ps(st, f"key_bank{i}", [P, N]) for i in range(2)]
        row_bank = [ps(st, f"row_bank{i}", [P, N]) for i in range(2)]
        proj_bank = [ps(st, f"proj_bank{i}", [P, N]) for i in range(2)]
        pv_bank = ps(st, "pv_bank", [P, N])
        sum_bank = ps(st, "sum_bank", [P, N])

        proj_ready = sem("proj_ready")
        proj_taken = {"act": sem("proj_taken_act"), "dve": sem("proj_taken_dve")}
        row_ready, row_taken = sem("row_ready"), sem("row_taken")
        consts_ready = sem("consts_ready")
        cond_copied = sem("cond_copied")
        h_hi, h_split, k_hi, q_hi = sem("h_hi"), sem("h_split"), sem("k_hi"), sem("q_hi")
        k_stacked = [sem(f"k_stacked{g}") for g in range(HKV)]
        q_stacked = [[sem(f"q_stacked{i}{r}") for r in range(R)] for i in range(2)]
        max_hi, max_stacked = sem("max_hi"), sem("max_stacked")
        keys_scored, exp_done, pv_done, pv_copied = sem("keys_scored"), sem("exp_done"), sem("pv_done"), sem("pv_copied")
        added, sums_ready, log_done, inverse_ready = sem("added"), sem("sums_ready"), sem("log_done"), sem("inverse_ready")
        sums_taken, refined_done, attn_scaled = sem("sums_taken"), sem("refined_done"), sem("attn_scaled")
        attn_hi, attn_split = sem("attn_hi"), sem("attn_split")
        gate_loaded, resid_loaded, x1_added = sem("gate_loaded"), sem("resid_loaded"), sem("x1_added")

        STACKED = 3 * 16

        def group_no(b, g):
            return b * HKV + g

        def tile_no(b, g, kt):
            return b * (HKV * TT) + (g * TT + kt)

        def exps_no(b, g, kt):
            return b * (HKV * TT * R) + (g * TT + kt) * R

        def queries_stacked(b, g):
            return b * (HKV // 2 * STACKED) + (g // 2 + 1) * STACKED

        def rowed(b, g, has_next):
            if g + 1 < HKV:
                return b, g + 1
            return (b + 1, 0) if has_next else None

        def sequences(eng, before, sequence, after):
            before()
            sequence(0, False, True)
            with eng.Fori(1, B - 1) as b:
                sequence(b, True, True)
            sequence(B - 1, True, False)
            after(B - 1)

        with nc.Block() as block:
            @block.sync
            def _(sp):
                def load_x(src, b):
                    sp.dma_start(xa[:, :, :], seq_dram(src, b)).then_inc(x_loaded, 16)

                def load_resid(b):
                    sp.dma_start(gate_now[:, :], gate_dram[bass.ds(b, 1), 0, :].partition_broadcast(P)
                                 .rearrange("p a d -> p (a d)")).then_inc(gate_loaded, 16)
                    sp.dma_start(resid[:, :, :], seq_dram(x, b)).then_inc(resid_loaded, 16)

                def store_x1(b):
                    sp.wait_ge(x1_added, b * TT + TT)
                    sp.dma_start(seq_dram(x1_dram, b), resid[:, :, :]).then_inc(x1_stored, 16)

                def stack_k(g):
                    for row, part in ((0, 0), (1, 0), (2, 1)):
                        sp.dma_start(as_f32(k_stack[HD * row:HD * row + HD, g, :]),
                                     as_f32(k_part[part][HD * g:HD * g + HD, :])).then_inc(k_stacked[g], 16)

                def stack_q(u, g, heads=range(R)):
                    if 0 in heads:
                        sp.wait_ge(proj_taken["dve"], u.taken(f"Q{g}"))
                    for r in heads:
                        for row, part in ((0, 0), (1, 1), (2, 0)):
                            sp.dma_start(as_f32(q_stack[HD * row:HD * row + HD, g, r, :]),
                                         as_f32(q_part[g % 2][part][HD * r:HD * r + HD, :])).then_inc(q_stacked[g % 2][r], 16)

                def stack_max(b, g):
                    sp.wait_ge(row_taken, row_no(b, g, ROWS) + 1)
                    for part in range(2):
                        row = as_f32(q_stack[STACK + part:STACK + part + 1, g, :, :])
                        sp.dma_start(row.rearrange("o r n -> o (r n)"), as_f32(max_row[part][:, :])).then_inc(max_stacked, 16)

                def before():
                    u = before_units()
                    sp.wait_ge(proj_taken["dve"], u.taken("K"))
                    stack_k(0)
                    stack_q(u, 0)
                    stack_k(1)
                    stack_q(u, 1)
                    stack_max(0, 0)
                    stack_k(2)
                    stack_k(3)

                def sequence(b, has_last, has_next):
                    u = seq_units(b, has_last, has_next)
                    if has_last:
                        sp.wait_ge(keys_scored, exps_no(b, 0, 0))
                        stack_k(HKV - 1)
                    if has_next:
                        load_x(x, b + 1)
                    else:
                        load_x(x1_dram, 0)
                    stack_q(u, 2)
                    stack_max(b, 1)
                    stack_q(u, 3)
                    stack_max(b, 2)
                    if has_last:
                        store_x1(b - 1)
                        sp.wait_ge(x1_stored, b * 16)
                    load_resid(b)
                    if has_next:
                        sp.wait_ge(proj_taken["dve"], u.taken("K"))
                        stack_k(0)
                        stack_k(1)
                    stack_max(b, 3)
                    if has_next:
                        stack_q(u, 0)
                        stack_q(u, 1)
                        stack_k(2)
                        stack_max(b + 1, 0)

                def after(b):
                    for g in range(HKV):
                        sp.wait_ge(k_stacked[g], b * STACKED + STACKED)
                        for i in range(2):
                            sp.wait_ge(q_stacked[i][g], queries_stacked(b, 2))
                    for j in range(RING):
                        load_weights(sp, j)
                    store_x1(b)

                sequences(sp, before, sequence, after)

            @block.gpsimd
            def _(pool):
                def rstd_of(b):
                    pool.wait_ge(eps_added, b + 1)
                    nc.gpsimd.tensor_tensor(rstd[:, :], var_eps[:, :], neg_half[:, :], ALU.pow).then_inc(rstd_ready, 1)

                def add_probs(b, g, kt):
                    pool.wait_ge(exp_done, exps_no(b, g, kt) + R)
                    if kt > 1:
                        pool.wait_ge(added, group_no(b, g) * (TT - 1) + (kt - 1))
                    first_in = probs[0] if kt == 1 else probs_sum
                    nc.gpsimd.tensor_tensor(probs_sum[:, :, :], first_in[:, :, :], probs[kt][:, :, :],
                                            ALU.add).then_inc(added, 1)

                def add_resid(b, tt, u):
                    if tt == 0:
                        pool.wait_ge(resid_loaded, b * 16 + 16)
                    pool.wait_ge(proj_taken["dve"], u.taken(f"O{tt}"))
                    nc.gpsimd.tensor_tensor(resid[:, tt, :], resid[:, tt, :], gated[tt % 2][:, :],
                                            ALU.add).then_inc(x1_added, 1)

                def before():
                    nc.gpsimd.memset(as_f32(k_stack[STACK:SHIFT, :, :]), 1.0).then_inc(consts_ready, 1)
                    pool.wait_ge(consts_ready, 1)
                    nc.gpsimd.memset(ones[:, :], 1.0).then_inc(consts_ready, 1)

                def sequence(b, has_last, has_next):
                    u = seq_units(b, has_last, has_next)
                    for g in range(HKV):
                        by_pool = has_next or g < HKV - 1
                        if (has_last or g > 0) and by_pool:
                            pool.wait_ge(sums_ready, group_no(b, g))
                        for kt in range(TT):
                            if kt > 0 and by_pool:
                                add_probs(b, g, kt)
                            if g == 1 and has_last:
                                add_resid(b - 1, kt, u)
                        if g == 0:
                            rstd_of(b + 1)

                def after(b):
                    for tt in range(TT):
                        add_resid(b, tt, after_units())

                sequences(pool, before, sequence, after)

            @block.scalar
            def _(act):
                def norm(b, tiles):
                    if 0 in tiles:
                        act.wait_ge(shift_ready, b + 1)
                    for tt in tiles:
                        nc.scalar.activation(xa[:, tt, :], xa[:, tt, :], ACT.Identity, scale=rstd[:, tt:tt + 1],
                                             bias=shift_col[:, tt:tt + 1]).then_inc(normed, 1)

                def modulate(b, u, tiles, is_first=False, scale=SC1, shift=SH1):
                    if 0 in tiles:
                        act.wait_ge(cond_copied, b + 1)
                    for kt in tiles:
                        act.wait_ge(proj_ready, u.ready(f"T{kt}"))
                        if not (is_first and kt < 2):
                            act.wait_ge(h_split, b * KD + (kt - 1))
                        nc.scalar.activation(h_full[kt % 2][:, :], proj_bank[u.bank(f"T{kt}")][:, :], ACT.Identity,
                                             scale=cond_now[:, scale + kt:scale + kt + 1],
                                             bias=cond_now[:, shift + kt:shift + kt + 1]).then_inc(proj_taken["act"], 1)
                        act.wait_ge(proj_taken["act"], u.taken(f"T{kt}"))
                        nc.scalar.activation(h[0][:, kt, :], h_full[kt % 2][:, :], ACT.Copy).then_inc(h_hi, 1)

                def k_high(b, u, is_first=False):
                    act.wait_ge(proj_ready, u.ready("K"))
                    if not is_first:
                        act.wait_ge(k_stacked[HKV - 1], b * STACKED)
                    nc.scalar.activation(k_part[0][:, :], proj_bank[u.bank("K")][:, :], ACT.Copy).then_inc(k_hi, 1)

                def q_high(b, g, u, is_first=False):
                    act.wait_ge(proj_ready, u.ready(f"Q{g}"))
                    if not (is_first and g < 2):
                        for r in range(R):
                            act.wait_ge(q_stacked[g % 2][r], queries_stacked(b, g) - STACKED)
                    nc.scalar.activation(q_part[g % 2][0][:, :], proj_bank[u.bank(f"Q{g}")][:, :], ACT.Copy,
                                         scale=SCORE_SCALE).then_inc(q_hi, 1)

                def take_v(u):
                    act.wait_ge(proj_ready, u.ready("V"))
                    nc.scalar.activation(v_full[:, :], proj_bank[u.bank("V")][:, :], ACT.Copy).then_inc(proj_taken["act"], 1)

                def take_vt(b, u, has_last):
                    act.wait_ge(proj_ready, u.ready("VT"))
                    if has_last:
                        act.wait_ge(pv_done, tile_no(b, 0, 0))
                    nc.scalar.activation(v[:, :, :].rearrange("p t n -> p (t n)"), proj_bank[u.bank("VT")][:, :],
                                         ACT.Copy).then_inc(proj_taken["act"], 1)

                def max_high(b, g, is_first=False):
                    n = row_no(b, g, ROWS)
                    act.wait_ge(row_ready, n + 1)
                    if not is_first:
                        act.wait_ge(max_stacked, group_no(b, g) * 32)
                    nc.scalar.activation(max_row[0][:, :], row_bank[g % 2][0:ROWS, 0:P], ACT.Copy).then_inc(max_hi, 1)

                def exp(b, g, kt, r, has_last):
                    if r == 0 and (has_last or g > 0):
                        act.wait_ge(pv_done, tile_no(b, g, kt) - (TT - 1))
                        act.wait_ge(added, group_no(b, g) * (TT - 1) - (TT - 1) + max(kt, 1))
                    act.wait_ge(keys_scored, exps_no(b, g, kt) + (r + 1))
                    nc.scalar.activation(probs[kt][:, r, :], key_bank[r % 2][:, :], ACT.Exp).then_inc(exp_done, 1)

                def copy_pv(b, g, is_first=False):
                    act.wait_ge(pv_done, tile_no(b, g, TT - 1) + 1)
                    if not is_first:
                        act.wait_ge(attn_scaled, group_no(b, g))
                    nc.scalar.activation(attn_raw[:, :], pv_bank[:, :], ACT.Copy).then_inc(pv_copied, 1)

                def invert(b, g, is_first=False):
                    n = group_no(b, g)
                    act.wait_ge(sums_ready, n + 1)
                    if not is_first:
                        act.wait_ge(refined_done, n)
                    nc.scalar.activation(inverse[:, :], sum_bank[:, :], ACT.Ln).then_inc(log_done, 1)
                    act.wait_ge(log_done, n + 1)
                    nc.scalar.activation(inverse[:, :], inverse[:, :], ACT.Exp, scale=-1.0).then_inc(inverse_ready, 1)

                def attn_high(b, g):
                    act.wait_ge(attn_scaled, group_no(b, g) + 1)
                    nc.scalar.activation(attn[0][:, g, :], attn_full[:, :], ACT.Copy).then_inc(attn_hi, 1)

                def before():
                    u = before_units()
                    modulate(0, u, range(KD), is_first=True)
                    k_high(0, u, is_first=True)
                    q_high(0, 0, u, is_first=True)
                    q_high(0, 1, u, is_first=True)
                    take_v(u)
                    max_high(0, 0, is_first=True)

                def slot(b, g, kt, u, has_last, has_next):
                    prev = (b, g - 1) if g > 0 else (b - 1, HKV - 1) if has_last else None
                    first_group = (g == 1 and not has_last)
                    exp(b, g, kt, 0, has_last)
                    if kt == TT - 1 and rowed(b, g, has_next):
                        max_high(*rowed(b, g, has_next))
                    exp(b, g, kt, 1, has_last)
                    if prev and kt == 0:
                        copy_pv(*prev, is_first=first_group)
                    if prev and kt == 2:
                        invert(*prev, is_first=first_group)
                    if (g, kt) == (2, 0):
                        if has_last:
                            act.wait_ge(proj_ready, u.ready("O3"))
                        attn_high(b, 0)
                    exp(b, g, kt, 2, has_last)
                    exp(b, g, kt, 3, has_last)
                    if prev and kt == 3 and g != 1:
                        attn_high(*prev)
                    if (g, kt) in ((1, 1), (1, 2)):
                        norm(b + 1, range(2 * kt - 2, 2 * kt))
                    for name in fill(g, kt, has_last, has_next):
                        if name == "VT":
                            take_vt(b, u, has_last)
                        elif name == "V":
                            take_v(u)
                        elif name[0] == "T":
                            if has_next:
                                modulate(b + 1, u, (int(name[1]),))
                            else:
                                modulate(b + 1, u, (int(name[1]),), scale=SC2, shift=SH2)
                        elif name == "K":
                            k_high(b + 1, u)
                        elif name[0] == "Q":
                            q_high(b if name in ("Q2", "Q3") else b + 1, int(name[1]), u)

                def sequence(b, has_last, has_next):
                    u = seq_units(b, has_last, has_next)
                    for g in range(HKV):
                        for kt in range(TT):
                            slot(b, g, kt, u, has_last, has_next)

                def after(b):
                    copy_pv(b, HKV - 1)
                    invert(b, HKV - 1)
                    attn_high(b, HKV - 1)

                sequences(act, before, sequence, after)

            @block.vector
            def _(dve):
                def copy_cond(b):
                    if isinstance(b, int):
                        b = b % B
                    nc.vector.tensor_copy(cond_now[:, :], cond_cols[:, bass.ds(b, 1), :]
                                          .rearrange("p a j -> p (a j)")).then_inc(cond_copied, 1)

                def tile_stats(tiles):
                    for tt in tiles:
                        nc.vector.bn_stats(stats[:, tt, :], xa[:, tt, :]).then_inc(stats_done, 1)

                def moments(b):
                    for tt in range(TT):
                        nc.vector.bn_aggr(mean_var[:, tt, :], stats[:, tt, :]).then_inc(moments_done, 1)
                    dve.wait_ge(moments_done, b * TT + TT)
                    nc.vector.tensor_scalar(var_eps[:, :], mean_var[:, :, 1], EPS, None, ALU.add).then_inc(eps_added, 1)

                def shift_of(b):
                    dve.wait_ge(rstd_ready, b + 1)
                    nc.vector.scalar_tensor_tensor(out=shift_col[:, :], in0=mean_var[:, :, 0], scalar=-1.0,
                                                   in1=rstd[:, :], op0=ALU.mult, op1=ALU.mult).then_inc(shift_ready, 1)

                def h_low(b, tiles):
                    for kt in tiles:
                        dve.wait_ge(h_hi, b * KD + (kt + 1))
                        nc.vector.tensor_tensor(h[1][:, kt, :], h_full[kt % 2][:, :], as_f32(h[0][:, kt, :]),
                                                ALU.subtract).then_inc(h_split, 1)

                def k_low(b, u):
                    dve.wait_ge(k_hi, b + 1)
                    nc.vector.tensor_tensor(k_part[1][:, :], proj_bank[u.bank("K")][:, :], as_f32(k_part[0][:, :]),
                                            ALU.subtract).then_inc(proj_taken["dve"], 1)

                def q_low(b, g, u):
                    dve.wait_ge(q_hi, group_no(b, g) + 1)
                    nc.vector.scalar_tensor_tensor(out=q_part[g % 2][1][:, :], in0=proj_bank[u.bank(f"Q{g}")][:, :],
                                                   scalar=SCORE_SCALE, in1=as_f32(q_part[g % 2][0][:, :]),
                                                   op0=ALU.mult, op1=ALU.subtract).then_inc(proj_taken["dve"], 1)

                def row_max(b, g, i):
                    dve.wait_ge(row_ready, row_no(b, g, i) + 1)
                    nc.vector.tensor_reduce(out=neg_max[:, g % 2, i:i + 1], in_=row_bank[(g + i) % 2][:, :], op=ALU.max,
                                            axis=AX.X, negate=True).then_inc(row_taken, 1)

                def max_low(b, g):
                    dve.wait_ge(max_hi, group_no(b, g) + 1)
                    nc.vector.tensor_tensor(max_row[1][:, :], row_bank[g % 2][0:ROWS, 0:P],
                                            as_f32(max_row[0][:, :]), ALU.subtract).then_inc(row_taken, 1)

                def refine(b, g):
                    n = group_no(b, g) + 1
                    dve.wait_ge(inverse_ready, n)
                    nc.vector.tensor_tensor(refined[:, :], sum_bank[:, :], inverse[:, :], ALU.mult).then_inc(sums_taken, 1)
                    dve.wait_ge(sums_taken, n)
                    nc.vector.scalar_tensor_tensor(out=refined[:, :], in0=refined[:, :], scalar=2.0, in1=inverse[:, :],
                                                   op0=ALU.subtract, op1=ALU.mult).then_inc(refined_done, 1)

                def divide(b, g):
                    n = group_no(b, g) + 1
                    dve.wait_ge(refined_done, n)
                    dve.wait_ge(pv_copied, n)
                    nc.vector.scalar_tensor_tensor(out=attn_full[:, :], in0=attn_raw[:, :], scalar=-1.0, in1=refined[:, :],
                                                   op0=ALU.mult, op1=ALU.mult).then_inc(attn_scaled, 1)

                def add_probs(b, g, kt):
                    if kt == 1:
                        dve.wait_ge(sums_ready, group_no(b, g))
                    else:
                        dve.wait_ge(added, group_no(b, g) * (TT - 1) + (kt - 1))
                    dve.wait_ge(exp_done, exps_no(b, g, kt) + R)
                    first_in = probs[0] if kt == 1 else probs_sum
                    nc.vector.tensor_tensor(probs_sum[:, :, :], first_in[:, :, :], probs[kt][:, :, :],
                                            ALU.add).then_inc(added, 1)

                def attn_low(b, g):
                    dve.wait_ge(attn_hi, group_no(b, g) + 1)
                    nc.vector.tensor_tensor(attn[1][:, g, :], attn_full[:, :], as_f32(attn[0][:, g, :]),
                                            ALU.subtract).then_inc(attn_split, 1)

                def gate(b, tt, u):
                    dve.wait_ge(proj_ready, u.ready(f"O{tt}"))
                    if tt == 0:
                        dve.wait_ge(gate_loaded, b * 16 + 16)
                    if tt >= 2:
                        dve.wait_ge(x1_added, b * TT + (tt - 1))
                    nc.vector.tensor_tensor(gated[tt % 2][:, :], proj_bank[u.bank(f"O{tt}")][:, :], gate_now[:, :],
                                            ALU.mult).then_inc(proj_taken["dve"], 1)

                def before():
                    u = before_units()
                    copy_cond(0)
                    h_low(0, range(KD))
                    k_low(0, u)
                    q_low(0, 0, u)
                    q_low(0, 1, u)
                    for i in range(ROWS):
                        row_max(0, 0, i)
                    max_low(0, 0)

                def finish(b, g, kt, u, has_last, has_next):
                    for name in fill(g, kt, has_last, has_next):
                        if name[0] == "T":
                            h_low(b + 1, (int(name[1]),))
                        elif name == "K":
                            k_low(b + 1, u)
                        elif name[0] == "Q":
                            q_low(b if name in ("Q2", "Q3") else b + 1, int(name[1]), u)
                        elif name[0] == "O":
                            gate(b - 1, int(name[1]), u)

                def norm_ahead(b, g, kt):
                    if (g, kt) == (0, 2):
                        dve.wait_ge(x_loaded, b * 16 + 32)
                        tile_stats((0, 1))
                    if (g, kt) == (0, 3):
                        tile_stats((2, 3))
                        dve.wait_ge(stats_done, b * TT + 2 * TT)
                        copy_cond(b + 1)
                        moments(b + 1)
                    if (g, kt) == (1, 1):
                        shift_of(b + 1)

                def slot(b, g, kt, u, has_last, has_next):
                    prev = (b, g - 1) if g > 0 else (b - 1, HKV - 1) if has_last else None
                    to_row = [(*rowed(b, g, has_next), i) for i in range(FIRST_ROW[g][kt], FIRST_ROW[g][kt] + ROWS_IN_SLOT[g][kt])
                              ] if rowed(b, g, has_next) else []
                    if kt == TT - 1 and rowed(b, g, has_next):
                        max_low(*rowed(b, g, has_next))
                    for row in to_row[:2]:
                        row_max(*row)
                    if prev and kt == 3:
                        divide(*prev)
                    if (g, kt) != (0, 0):
                        finish(b, *((g, kt - 1) if kt > 0 else (g - 1, TT - 1)), u, has_last, has_next)
                    for row in to_row[2:4]:
                        row_max(*row)
                    norm_ahead(b, g, kt)
                    if prev and kt == 2:
                        refine(*prev)
                    if prev and kt == 3 and g != 1:
                        attn_low(*prev)
                    if (g, kt) == (2, 1):
                        attn_low(b, 0)
                    for row in to_row[4:]:
                        row_max(*row)
                    if g == HKV - 1 and not has_next and kt > 0:
                        add_probs(b, g, kt)

                def sequence(b, has_last, has_next):
                    u = seq_units(b, has_last, has_next)
                    for g in range(HKV):
                        for kt in range(TT):
                            slot(b, g, kt, u, has_last, has_next)

                def after(b):
                    refine(b, HKV - 1)
                    divide(b, HKV - 1)
                    attn_low(b, HKV - 1)
                    for tt in range(TT):
                        gate(b, tt, after_units())

                sequences(dve, before, sequence, after)

            @block.tensor
            def _(pe):
                def room(u, name):
                    i = u.at[name]
                    if i >= 2:
                        back = u.order[i - 2]
                        pe.wait_ge(proj_taken[TAKER[back[0]]], u.taken(back))
                    elif not (isinstance(u.base["all"], int) and u.base["all"] == 0):
                        for who in ("act", "dve"):
                            pe.wait_ge(proj_taken[who], u.base[who])
                    return proj_bank[u.bank(name)]

                def product(bank, lhs, rhs, half):
                    part_product(bank, lhs, rhs, range(KD // 2 * half, KD // 2 * (half + 1)))

                def part_product(bank, lhs, rhs, tiles):
                    for kt in tiles:
                        for i, j in ((0, 0), (0, 1), (1, 0)):
                            last = nc.tensor.matmul(bank, lhs(i, kt), rhs(j, kt), start=(kt == 0 and (i, j) == (0, 0)),
                                                    stop=(kt == KD - 1 and (i, j) == (1, 0)))
                    if KD - 1 in tiles:
                        last.then_inc(proj_ready, 1)

                def turn_x(b, kt, u):
                    bank = room(u, f"T{kt}")
                    for tt in range(TT):
                        if kt == 0:
                            pe.wait_ge(normed, b * TT + (tt + 1))
                        last = nc.tensor.transpose(bank[:, tt * P:tt * P + P], xa[:, tt, kt * P:kt * P + P], ident[:, :])
                    last.then_inc(proj_ready, 1)

                def turn_v(u, v_taken):
                    bank = room(u, "VT")
                    pe.wait_ge(proj_taken["act"], v_taken)
                    for tt in range(TT):
                        last = nc.tensor.transpose(bank[:, tt * P:tt * P + P], v_full[:, tt * P:tt * P + P], ident[:, :])
                    last.then_inc(proj_ready, 1)

                def project_k(b, u, half):
                    if half == 0:
                        room(u, "K")
                    pe.wait_ge(h_split, b * KD + KD // 2 * (half + 1))
                    product(proj_bank[u.bank("K")][:, :], lambda i, kt: wk_t[i][:, kt, :], lambda j, kt: h[j][:, kt, :], half)

                def project_q(g, u, half):
                    if half == 0:
                        room(u, f"Q{g}")
                    product(proj_bank[u.bank(f"Q{g}")][:, :], lambda i, kt: wq_t[i][:, kt, g * P:g * P + P],
                            lambda j, kt: h[j][:, kt, :], half)

                def project_v(u, half):
                    if half == 0:
                        room(u, "V")
                    product(proj_bank[u.bank("V")][:, :], lambda i, kt: wv_t[i][:, kt, :], lambda j, kt: h[j][:, kt, :], half)

                def project_out(b, tt, u, half):
                    out_part(b, tt, u, range(KD // 2 * half, KD // 2 * (half + 1)))

                def out_part(b, tt, u, groups):
                    if 0 in groups:
                        room(u, f"O{tt}")
                    if tt == 0 or HKV - 1 in groups:
                        pe.wait_ge(attn_split, b * HKV + (max(groups) + 1))
                    part_product(proj_bank[u.bank(f"O{tt}")][:, :], lambda i, g: attn[i][:, g, tt * P:tt * P + P],
                                 lambda j, g: wo_t[j][:, g, :], groups)

                def rows(b, g, i):
                    if i == 0:
                        pe.wait_ge(k_stacked[g], b * STACKED + STACKED)
                    if i % TT == 0:
                        pe.wait_ge(q_stacked[g % 2][i // TT], queries_stacked(b, g))
                    if not (isinstance(b, int) and b == 0 and g == 0 and i < 2):
                        pe.wait_ge(row_taken, row_no(b, g, i) - 1)
                    r, qt = i // TT, i % TT
                    nc.tensor.matmul(row_bank[(g + i) % 2][:, :], q_stack[0:STACK, g, r, qt * P:qt * P + P],
                                     k_stack[0:STACK, g, :], start=True, stop=True).then_inc(row_ready, 1)

                def turn_max(b, g):
                    pe.wait_ge(row_taken, row_no(b, g, ROWS))
                    nc.tensor.transpose(row_bank[g % 2][0:ROWS, 0:P], neg_max[:, g % 2, :], ident[:, :]).then_inc(row_ready, 1)

                def scores(b, g, kt, r, has_last):
                    if kt == 0 and r == 0:
                        pe.wait_ge(max_stacked, group_no(b, g) * 32 + 32)
                    if has_last or g > 0 or kt > 0 or r >= 2:
                        pe.wait_ge(exp_done, exps_no(b, g, kt) + (r - 1))
                    nc.tensor.matmul(key_bank[r % 2][:, :], k_stack[0:SHIFT, g, kt * P:kt * P + P],
                                     q_stack[0:SHIFT, g, r, :], start=True, stop=True).then_inc(keys_scored, 1)

                def values(b, g, kt, is_first=False):
                    pe.wait_ge(exp_done, exps_no(b, g, kt) + R)
                    if kt == 0 and not is_first:
                        pe.wait_ge(pv_copied, group_no(b, g))
                    for r in range(R):
                        last = nc.tensor.matmul(pv_bank[HD * r:HD * r + HD, :], v[:, kt, g * HD:g * HD + HD],
                                                probs[kt][:, r, :], start=(kt == 0), stop=(kt == TT - 1))
                    last.then_inc(pv_done, 1)

                def sums(b, g, is_first=False):
                    pe.wait_ge(added, group_no(b, g) * (TT - 1) + (TT - 1))
                    if not is_first:
                        pe.wait_ge(sums_taken, group_no(b, g))
                    for r in range(R):
                        last = nc.tensor.matmul(sum_bank[HD * r:HD * r + HD, :], ones[:, :], probs_sum[:, r, :],
                                                start=True, stop=True)
                    last.then_inc(sums_ready, 1)

                def before():
                    u = before_units()
                    for kt in range(KD):
                        turn_x(0, kt, u)
                    for half in range(2):
                        project_k(0, u, half)
                    for g in range(2):
                        for half in range(2):
                            project_q(g, u, half)
                    for half in range(2):
                        project_v(u, half)
                    pe.wait_ge(consts_ready, 2)
                    for i in range(ROWS):
                        rows(0, 0, i)
                    turn_max(0, 0)

                def do(name, half, b, u):
                    if name == "VT":
                        turn_v(u, u.base["act"])
                    elif name[0] == "T":
                        turn_x(b + 1, int(name[1]), u)
                    elif name == "K":
                        project_k(b + 1, u, half)
                    elif name == "V":
                        project_v(u, half)
                    elif name[0] == "Q":
                        project_q(int(name[1]), u, half)
                    else:
                        project_out(b - 1, int(name[1]), u, half)

                def slot(b, g, kt, u, has_last, has_next):
                    prev = (b, g - 1) if g > 0 else (b - 1, HKV - 1) if has_last else None
                    parts = [(name, half) for name in fill(g, kt, has_last, has_next)
                             for half in ((0,) if name[0] == "T" or name == "VT" else (0, 1))]
                    cut = (len(parts) + 1) // 2
                    to_row = list(range(FIRST_ROW[g][kt], FIRST_ROW[g][kt] + ROWS_IN_SLOT[g][kt])) if rowed(b, g, has_next) else []

                    def some_rows(n):
                        for _ in range(min(n, len(to_row))):
                            rows(*rowed(b, g, has_next), to_row.pop(0))

                    scores(b, g, kt, 0, has_last)
                    if kt == TT - 1 and rowed(b, g, has_next):
                        turn_max(*rowed(b, g, has_next))
                    scores(b, g, kt, 1, has_last)
                    late = (g, kt) == (3, 0)
                    some_rows(0 if late else 2 if len(to_row) > 5 else 1)
                    if kt > 0:
                        if (g, kt) == (0, 1):
                            pe.wait_ge(proj_taken["act"], u.taken("VT"))
                        values(b, g, kt - 1, is_first=not has_last and g == 0)
                    elif prev:
                        values(*prev, TT - 1)
                    some_rows(0 if late else 1)
                    scores(b, g, kt, 2, has_last)
                    scores(b, g, kt, 3, has_last)
                    some_rows(1)
                    for name, half in parts[:cut]:
                        do(name, half, b, u)
                    some_rows(1)
                    for name, half in parts[cut:]:
                        do(name, half, b, u)
                    if kt == 1 and prev:
                        sums(*prev, is_first=not has_last and g == 1)
                    some_rows(len(to_row))

                def sequence(b, has_last, has_next):
                    u = seq_units(b, has_last, has_next)
                    for g in range(HKV):
                        for kt in range(TT):
                            slot(b, g, kt, u, has_last, has_next)

                def after(b):
                    u = after_units()
                    values(b, HKV - 1, TT - 1)
                    for tt in range(2):
                        out_part(b, tt, u, range(HKV - 1))
                    sums(b, HKV - 1)
                    for tt in range(2):
                        out_part(b, tt, u, range(HKV - 1, HKV))
                    for tt in range(2, TT):
                        out_part(b, tt, u, range(HKV))

                sequences(pe, before, sequence, after)


def mlp(nc, f32, f32r, ALU, ACT, sb, ps, sem, as_f32, seq_dram, ident, cond_cols, bias_cols, neg_half, norm_bufs,
        spare, resid, gate_now, x1_stored, w_loaded, load_weights, b2, x1_dram, gate_dram, out):
    xb, stats, mean_var, var_eps, rstd, shift_col, cond_now, h_full, h = norm_bufs
    with ExitStack() as st:
        w1_t = [sb(st, f"w1_t{i}", [P, KD, DFF], f32r) for i in range(2)]
        w2_t = [sb(st, f"w2_t{i}", [P, NJ, D], f32r) for i in range(2)]
        gelu_full = [sb(st, f"gelu_full{i}", [P, N]) for i in range(2)]
        hidden = [[sb(st, f"hidden{s}{i}", [P, N], f32r) for i in range(2)] for s in range(2)]
        y = sb(st, "y", [P, TT, D])
        b2_rows = sb(st, "b2_rows", [P, D])

        acc = [ps(st, f"acc{i}", [P, D]) for i in range(TT)]
        up = [ps(st, f"up{i}", [P, N]) for i in range(2)]
        turn = [ps(st, f"turn{i}", [P, N]) for i in range(2)]

        w1_in, w2_in = [as_f32(slot[0][:, :]) for slot in spare], [as_f32(slot[1][:, :]) for slot in spare]
        x_loaded, stats_done, moments_done, eps_added = sem("x_loaded2"), sem("stats_done2"), sem("moments_done2"), sem("eps_added2")
        rstd_ready, shift_ready, normed, cond_copied = sem("rstd_ready2"), sem("shift_ready2"), sem("normed2"), sem("cond_copied2")
        turned, h_ready, h_hi, h_split = sem("turned"), sem("h_ready2"), sem("h_hi2"), sem("h_split2")
        w_turned, w_hi, w_split = sem("w_turned2"), sem("w_hi2"), sem("w_split2")
        up_ready, gelu_done, hid_hi, hid_split, down_done = sem("up_ready"), sem("gelu_done"), sem("hid_hi"), sem("hid_split"), sem("down_done")
        acc_ready, acc_taken, y_gated, y_added = sem("acc_ready"), sem("acc_taken"), sem("y_gated"), sem("y_added")
        b2_loaded, gate_loaded, resid_loaded, out_stored = sem("b2_loaded"), sem("gate_loaded2"), sem("resid_loaded2"), sem("out_stored")

        def sequences(eng, body):
            body(0, True, True)
            with eng.Fori(1, B - 1) as b:
                body(b, False, True)
            body(B - 1, False, False)

        with nc.Block() as block:
            @block.sync
            def _(sp):
                def body(b, is_first, has_next):
                    if is_first:
                        sp.dma_start(b2_rows[:, :], b2.rearrange("(a d) -> a d", a=1).partition_broadcast(P).rearrange("p a d -> p (a d)")).then_inc(b2_loaded, 16)
                        load_next(b, is_first)
                        for j in range(RING, NJ):
                            sp.wait_ge(w_turned, 2 * (j - RING) + 2)
                            load_weights(sp, j)
                        sp.wait_ge(x1_stored, B * 16)
                    elif has_next:
                        load_next(b, is_first)
                    if not is_first:
                        store(b - 1)
                    sp.dma_start(gate_now[:, :], gate_dram[bass.ds(b, 1), 1, :].partition_broadcast(P).rearrange("p a d -> p (a d)")).then_inc(gate_loaded, 16)
                    sp.dma_start(resid[:, :, :], seq_dram(x1_dram, b)).then_inc(resid_loaded, 16)
                    if not has_next:
                        store(b)

                def load_next(b, is_first):
                    if not is_first:
                        sp.wait_ge(turned, b * KD)
                    sp.dma_start(xb[:, :, :], seq_dram(x1_dram, b + 1)).then_inc(x_loaded, 16)

                def store(b):
                    sp.wait_ge(y_added, b * TT + TT)
                    sp.dma_start(seq_dram(out, b), y[:, :, :]).then_inc(out_stored, 16)
                    sp.wait_ge(out_stored, b * 16 + 16)

                sequences(sp, body)

            @block.gpsimd
            def _(pool):
                def next_rstd(b):
                    pool.wait_ge(eps_added, b + 1)
                    nc.gpsimd.tensor_tensor(rstd[:, :], var_eps[:, :], neg_half[:, :], ALU.pow).then_inc(rstd_ready, 1)

                def body(b, is_first, has_next):
                    if has_next:
                        next_rstd(b)
                    pool.wait_ge(gate_loaded, b * 16 + 16)
                    pool.wait_ge(resid_loaded, b * 16 + 16)
                    for tt in range(TT):
                        n = b * TT + (tt + 1)
                        pool.wait_ge(acc_taken, n)
                        nc.gpsimd.tensor_tensor(y[:, tt, :], y[:, tt, :], gate_now[:, :], ALU.mult).then_inc(y_gated, 1)
                        pool.wait_ge(y_gated, n)
                        nc.gpsimd.tensor_tensor(y[:, tt, :], y[:, tt, :], resid[:, tt, :], ALU.add).then_inc(y_added, 1)

                sequences(pool, body)

            @block.scalar
            def _(act):
                def norm_next(b):
                    act.wait_ge(shift_ready, b + 1)
                    for tt in range(TT):
                        nc.scalar.activation(xb[:, tt, :], xb[:, tt, :], ACT.Identity, scale=rstd[:, tt:tt + 1],
                                             bias=shift_col[:, tt:tt + 1]).then_inc(normed, 1)

                def modulate_next(b, kt, is_first):
                    if kt == 0:
                        act.wait_ge(cond_copied, b + 1)
                    act.wait_ge(turned, b * KD + (kt + 1))
                    if not (is_first and kt < 2):
                        act.wait_ge(h_split, b * KD + (kt - 1))
                    nc.scalar.activation(h_full[kt % 2][:, :], turn[kt % 2][:, :], ACT.Identity,
                                         scale=cond_now[:, SC2 + kt:SC2 + kt + 1],
                                         bias=cond_now[:, SH2 + kt:SH2 + kt + 1]).then_inc(h_ready, 1)

                def weights_high(j):
                    act.wait_ge(w_turned, 2 * j + 1)
                    nc.scalar.activation(w1_t[0][:, :, j * P:j * P + P], turn[0][:, :].rearrange("p (k n) -> p k n", k=KD),
                                         ACT.Copy).then_inc(w_hi, 1)
                    act.wait_ge(w_turned, 2 * j + 2)
                    nc.scalar.activation(w2_t[0][:, j, :], turn[1][:, :], ACT.Copy).then_inc(w_hi, 1)

                def body(b, is_first, has_next):
                    if is_first:
                        weights_high(0)
                    for j in range(NJ):
                        t = b * NJ + j
                        if is_first and j + 1 < NJ:
                            weights_high(j + 1)
                        act.wait_ge(up_ready, t + 1)
                        if not (is_first and j < 2):
                            act.wait_ge(hid_split, t - 1)
                        nc.scalar.activation(gelu_full[j % 2][:, :], up[j % 2][:, :], ACT.Gelu,
                                             bias=bias_cols[:, j:j + 1]).then_inc(gelu_done, 1)
                        if has_next and j == 9:
                            norm_next(b)
                        if has_next and j >= NJ - 2:
                            for kt in range((j - NJ + 2) * 2, (j - NJ + 2) * 2 + 2):
                                modulate_next(b, kt, is_first)

                sequences(act, body)

            @block.vector
            def _(dve):
                def next_tile_stats(b):
                    nc.vector.tensor_copy(cond_now[:, :], cond_cols[:, bass.ds(b + 1, 1), :].rearrange("p a j -> p (a j)")).then_inc(cond_copied, 1)
                    dve.wait_ge(x_loaded, b * 16 + 16)
                    for tt in range(TT):
                        nc.vector.bn_stats(stats[:, tt, :], xb[:, tt, :]).then_inc(stats_done, 1)

                def next_moments(b):
                    for tt in range(TT):
                        nc.vector.bn_aggr(mean_var[:, tt, :], stats[:, tt, :]).then_inc(moments_done, 1)
                    dve.wait_ge(moments_done, b * TT + TT)
                    nc.vector.tensor_scalar(var_eps[:, :], mean_var[:, :, 1], EPS, None, ALU.add).then_inc(eps_added, 1)

                def next_shift(b):
                    dve.wait_ge(rstd_ready, b + 1)
                    nc.vector.scalar_tensor_tensor(out=shift_col[:, :], in0=mean_var[:, :, 0], scalar=-1.0,
                                                   in1=rstd[:, :], op0=ALU.mult, op1=ALU.mult).then_inc(shift_ready, 1)

                def split_next_h(b, kt):
                    n = b * KD + (kt + 1)
                    dve.wait_ge(h_ready, n)
                    nc.vector.tensor_copy(h[0][:, kt, :], h_full[kt % 2][:, :]).then_inc(h_hi, 1)
                    dve.wait_ge(h_hi, n)
                    nc.vector.tensor_tensor(h[1][:, kt, :], h_full[kt % 2][:, :], as_f32(h[0][:, kt, :]),
                                            ALU.subtract).then_inc(h_split, 1)

                def weights_low(j):
                    dve.wait_ge(w_hi, 2 * j + 1)
                    nc.vector.tensor_tensor(w1_t[1][:, :, j * P:j * P + P], turn[0][:, :].rearrange("p (k n) -> p k n", k=KD),
                                            as_f32(w1_t[0][:, :, j * P:j * P + P]), ALU.subtract).then_inc(w_split, 1)
                    dve.wait_ge(w_hi, 2 * j + 2)
                    nc.vector.tensor_tensor(w2_t[1][:, j, :], turn[1][:, :], as_f32(w2_t[0][:, j, :]),
                                            ALU.subtract).then_inc(w_split, 1)

                def split_hidden(b, j, is_first):
                    n = b * NJ + (j + 1)
                    dve.wait_ge(gelu_done, n)
                    if j >= 2:
                        dve.wait_ge(down_done, b * (NJ - 1) + (j - 1))
                    elif not is_first:
                        dve.wait_ge(*((down_done, b * (NJ - 1)) if j == 0 else (acc_ready, b * TT)))
                    nc.vector.tensor_copy(hidden[j % 2][0][:, :], gelu_full[j % 2][:, :]).then_inc(hid_hi, 1)
                    dve.wait_ge(hid_hi, n)
                    nc.vector.tensor_tensor(hidden[j % 2][1][:, :], gelu_full[j % 2][:, :], as_f32(hidden[j % 2][0][:, :]),
                                            ALU.subtract).then_inc(hid_split, 1)

                def take_acc(b, is_first):
                    if not is_first:
                        dve.wait_ge(out_stored, b * 16)
                    for tt in range(TT):
                        dve.wait_ge(acc_ready, b * TT + (tt + 1))
                        nc.vector.tensor_tensor(y[:, tt, :], acc[tt][:, :], b2_rows[:, :], ALU.add).then_inc(acc_taken, 1)

                def body(b, is_first, has_next):
                    if is_first:
                        weights_low(0)
                        dve.wait_ge(b2_loaded, 16)
                    for j in range(NJ):
                        if is_first and j + 1 < NJ:
                            weights_low(j + 1)
                        if has_next and j == 6:
                            dve.wait_ge(stats_done, b * TT + TT)
                        split_hidden(b, j, is_first)
                        if has_next and j == 5:
                            next_tile_stats(b)
                        if has_next and j == 6:
                            next_moments(b)
                        if has_next and j == 8:
                            next_shift(b)
                    if has_next:
                        dve.wait_ge(up_ready, b * NJ + NJ)
                        for kt in range(KD):
                            split_next_h(b, kt)
                    take_acc(b, is_first)

                sequences(dve, body)

            @block.tensor
            def _(pe):
                PASSES = ((0, 0), (0, 1), (1, 0))

                def turn_next_x(b, kt, is_first):
                    if kt >= 2:
                        pe.wait_ge(h_ready, b * KD + (kt - 1))
                    else:
                        if not is_first:
                            pe.wait_ge(h_ready, b * KD)
                        pe.wait_ge(w_split, 2 * NJ)
                    for tt in range(TT):
                        if kt == 0:
                            pe.wait_ge(normed, b * TT + (tt + 1))
                        last = nc.tensor.transpose(turn[kt % 2][:, tt * P:tt * P + P], xb[:, tt, kt * P:kt * P + P], ident[:, :])
                    last.then_inc(turned, 1)

                def turn_weights(j):
                    pe.wait_ge(w_loaded[j % RING], 32 * (j // RING) + 32)
                    if j > 0:
                        pe.wait_ge(w_split, 2 * j - 1)
                    for kt in range(KD):
                        last = nc.tensor.transpose(turn[0][:, kt * P:kt * P + P], w1_in[j % RING][:, kt * P:kt * P + P], ident[:, :])
                    last.then_inc(w_turned, 1)
                    if j > 0:
                        pe.wait_ge(w_split, 2 * j)
                    for o in range(KD):
                        last = nc.tensor.transpose(turn[1][:, o * P:o * P + P], w2_in[j % RING][:, o * P:o * P + P], ident[:, :])
                    last.then_inc(w_turned, 1)

                def up_product(b, j, is_first):
                    if is_first:
                        pe.wait_ge(w_split, 2 * j + 2)
                    if not (is_first and j < 2):
                        pe.wait_ge(gelu_done, b * NJ + (j - 1))
                    for kt in range(KD):
                        if j == 0 and not is_first:
                            pe.wait_ge(h_split, b * KD - KD + (kt + 1))
                        for n, (i, k) in enumerate(PASSES):
                            last = nc.tensor.matmul(up[j % 2][:, :], w1_t[i][:, kt, j * P:j * P + P], h[k][:, kt, :],
                                                    start=(kt == 0 and n == 0), stop=(kt == KD - 1 and n == 2))
                    last.then_inc(up_ready, 1)

                def down_product(b, j, is_first):
                    pe.wait_ge(hid_split, b * NJ + (j + 1))
                    for tt in range(TT):
                        if j == 0 and not is_first:
                            pe.wait_ge(acc_taken, b * TT - TT + (tt + 1))
                        for n, (i, k) in enumerate(PASSES):
                            last = nc.tensor.matmul(acc[tt][:, :], hidden[j % 2][i][:, tt * P:tt * P + P], w2_t[k][:, j, :],
                                                    start=(j == 0 and n == 0), stop=(j == NJ - 1 and n == 2))
                        if j == NJ - 1:
                            last.then_inc(acc_ready, 1)
                    if j < NJ - 1:
                        last.then_inc(down_done, 1)

                def body(b, is_first, has_next):
                    if is_first:
                        turn_weights(0)
                    for j in range(NJ):
                        if is_first and j + 1 < NJ:
                            turn_weights(j + 1)
                        up_product(b, j, is_first)
                        if j >= 1:
                            down_product(b, j - 1, is_first)
                        if has_next and j >= NJ - 2:
                            for kt in range((j - NJ + 2) * 2, (j - NJ + 2) * 2 + 2):
                                turn_next_x(b, kt, is_first)
                    down_product(b, NJ - 1, is_first)

                sequences(pe, body)


_INS = ["x", "cond_1024", "L0_cond_wq", "L0_cond_wk", "L0_cond_wv", "L0_cond_wo", "L0_cond_w1", "L0_cond_b1",
        "L0_cond_w2", "L0_cond_b2", "L0_cond_wc", "L0_cond_bc"]


def kernel(**inputs):
    import numpy as _np
    import concourse.bacc as _bacc
    from concourse import mybir as _mybir
    from concourse.bass_utils import run_bass_kernel_spmd as _run

    nc = _bacc.Bacc("TRN2", target_bir_lowering=False, num_devices=1)
    arrays, args = {}, []
    for name in _INS:
        a = _np.ascontiguousarray(inputs[name])
        arrays[f"in_{name}_dram"] = a
        args.append(nc.dram_tensor(f"in_{name}_dram", a.shape, _mybir.dt.from_np(a.dtype), kind="ExternalInput").ap())
    out = nc.dram_tensor("out_0_dram", (B, N, D), _mybir.dt.float32, kind="ExternalOutput").ap()
    layer_kernel(nc, *args, out)
    r = _run(nc, [arrays], core_ids=[0])
    return r.results[0]["out_0_dram"]
```
